# Optimizing a Trainium2 kernel written in Bass

```python
import numpy as np
import jax
import jax.numpy as jnp

def _softmax(x, axis=-1):
    return jax.nn.softmax(x, axis=axis)

def _gelu(x):
    return jax.nn.gelu(x, approximate=True)

def _silu(x):
    return jax.nn.silu(x)

def _sigmoid(x):
    return jax.nn.sigmoid(x)

def _layernorm(x, axis=-1, eps=1e-05):
    m = jnp.mean(x, axis=axis, keepdims=True)
    v = jnp.var(x, axis=axis, keepdims=True)
    return (x - m) / jnp.sqrt(v + eps)

def _scatter_add(tgt, idx, src, axis=0):
    return tgt.at[idx].add(src)

def _segment_sum(src, seg, n):
    return jax.ops.segment_sum(src, seg, n)
kernel_name = 'mk_lm_tower_d1_tok_ids768_r4_a68ae3'

def setup_inputs(seed: int=0):
    np.random.seed(seed)
    _w = jnp.asarray

    def _rec_inputs():
        import jax
        import jax.numpy as jnp
        _rk = jax.random.key(seed)
        x = jax.random.randint(jax.random.fold_in(_rk, 1), (2, 2048), 0, 31999, jnp.int32)
        mask_BS_i2_0 = jnp.where(jnp.ones((2, 2048), dtype=bool), 2, 0).astype(jnp.int32)
        return (x, mask_BS_i2_0)
    x, mask_BS_i2_0 = _rec_inputs()

    def _L0_tok_setup():
        import jax, jax.numpy as jnp
        import numpy as np
        VOCAB = 8000
        DIM = 192
        BATCH = 8
        SEQ = 512

        def _sinusoidal_pos(seq_len, dim):
            pos = jnp.arange(seq_len, dtype=jnp.float32)[:, None]
            ids = jnp.arange(dim, dtype=jnp.float32)[None, :]
            even_exp = jnp.floor(ids / 2.0) * 2.0 / dim
            angle = pos / jnp.power(10000.0, even_exp)
            return jnp.where(jnp.arange(dim) % 2 == 0, jnp.sin(angle), jnp.cos(angle))
        key = jax.random.key(seed)
        k1, k2, k3, k4 = jax.random.split(key, 4)
        input_tensor = jax.random.randint(k1, (BATCH, SEQ), 0, VOCAB)
        segment_label = jax.random.randint(k2, (BATCH, SEQ), 0, 3)
        token_table = jax.random.normal(k3, (VOCAB, DIM), dtype=jnp.float32) * 0.02
        segm_table = jax.random.normal(k4, (3, DIM), dtype=jnp.float32) * 0.02
        token_table = token_table.at[0].set(0.0)
        segm_table = segm_table.at[0].set(0.0)
        return {'input_tensor': input_tensor, 'segment_label': segment_label, 'token_table': token_table, 'segm_table': segm_table}
    _L0_tok_all = _L0_tok_setup()
    _L0_tok_in = {k: v for k, v in _L0_tok_all.items() if k in ('token_table', 'segm_table')}
    del _L0_tok_all

    def _L0_attn_setup():
        import jax, jax.numpy as jnp
        import numpy as np
        ROPE_THETA = 10000.0

        def rope(x):
            B, S, D = x.shape
            half = D // 2
            inv_freq = 1.0 / ROPE_THETA ** (jnp.arange(half, dtype=jnp.float32) * 2.0 / D)
            ang = jnp.arange(S, dtype=jnp.float32)[:, None] * inv_freq[None, :]
            cos, sin = (jnp.cos(ang), jnp.sin(ang))
            x1, x2 = (x[..., 0::2], x[..., 1::2])
            r1 = x1 * cos - x2 * sin
            r2 = x1 * sin + x2 * cos
            return jnp.stack([r1, r2], axis=-1).reshape(B, S, D)
        key = jax.random.key(seed)
        ks = jax.random.split(key, 9)
        B, S, D = (4, 512, 192)
        w = 0.02
        return {'X': jax.random.normal(ks[0], (B, S, D), dtype=jnp.float32), 'Wq': jax.random.normal(ks[1], (D, D), dtype=jnp.float32) * w, 'bq': jnp.zeros((D,), dtype=jnp.float32), 'Wk': jax.random.normal(ks[2], (D, D), dtype=jnp.float32) * w, 'bk': jnp.zeros((D,), dtype=jnp.float32), 'Wv': jax.random.normal(ks[3], (D, D), dtype=jnp.float32) * w, 'bv': jnp.zeros((D,), dtype=jnp.float32), 'Wo': jax.random.normal(ks[4], (D, D), dtype=jnp.float32) * w, 'bo': jnp.zeros((D,), dtype=jnp.float32)}
    _L0_attn_all = _L0_attn_setup()
    _L0_attn_in = {k: v for k, v in _L0_attn_all.items() if k in ('Wq', 'bq', 'Wk', 'bk', 'Wv', 'bv', 'Wo', 'bo')}
    del _L0_attn_all

    def _L0_ffn_setup():
        import jax, jax.numpy as jnp
        import numpy as np
        B, N, D, E = (2, 512, 192, 8)
        H = 4 * D
        TARGET_SPARSITY = 0.6
        K_KEEP = int(N * (1.0 - TARGET_SPARSITY))
        V_MAX, FEAT_CLAMP, ETA = (3.0, 10.0, 1.0)

        def _bk_gii(v):
            dr, di = (v, jnp.full_like(v, -ETA))

            def cf(reverse):
                init = (jnp.full((v.shape[0],), 1e+18, v.dtype), jnp.zeros((v.shape[0],), v.dtype))

                def step(c, d):
                    ar, ai = c
                    drr, dii = d
                    den = ar * ar + ai * ai
                    out = (drr - ar / den, dii + ai / den)
                    return (out, out)
                _, (r, i) = jax.lax.scan(step, init, (dr.T, di.T), reverse=reverse)
                return (r.T, i.T)
            ar, ai = cf(False)
            br, bi = cf(True)
            cr, ci = (ar + br - dr, ai + bi - di)
            den = cr * cr + ci * ci
            return (cr / den, -ci / den)
        key = jax.random.key(seed)
        ks = jax.random.split(key, 8)
        s = 0.02
        return {'x': jax.random.normal(ks[0], (B, N, D), jnp.float32), 'Wg': jax.random.normal(ks[1], (D, E), jnp.float32) * s, 'bg': jnp.zeros((E,), jnp.float32), 'W1': jax.random.normal(ks[2], (E, D, H), jnp.float32) * s, 'b1': jnp.zeros((E, H), jnp.float32), 'W2': jax.random.normal(ks[3], (E, H, D), jnp.float32) * s, 'b2': jnp.zeros((E, D), jnp.float32), 'Wv': jax.random.normal(ks[4], (D,), jnp.float32) * s, 'bv': jnp.zeros((), jnp.float32), 'Wm': jax.random.normal(ks[5], (D,), jnp.float32) * s, 'bm': jnp.zeros((), jnp.float32), 'Wo': jax.random.normal(ks[6], (2, D), jnp.float32) * s, 'bo': jnp.zeros((D,), jnp.float32), 'bk_scale': jnp.ones((), jnp.float32)}
    _L0_ffn_all = _L0_ffn_setup()
    _L0_ffn_in = {k: v for k, v in _L0_ffn_all.items() if k in ('Wg', 'bg', 'W1', 'b1', 'W2', 'b2', 'Wv', 'bv', 'Wm', 'bm', 'Wo', 'bo', 'bk_scale')}
    del _L0_ffn_all
    return {'x': x, 'mask_BS_i2_0': mask_BS_i2_0, 'L0_tok_token_table': _L0_tok_in['token_table'], 'L0_tok_segm_table': _L0_tok_in['segm_table'], 'L0_attn_Wq': _L0_attn_in['Wq'], 'L0_attn_bq': _L0_attn_in['bq'], 'L0_attn_Wk': _L0_attn_in['Wk'], 'L0_attn_bk': _L0_attn_in['bk'], 'L0_attn_Wv': _L0_attn_in['Wv'], 'L0_attn_bv': _L0_attn_in['bv'], 'L0_attn_Wo': _L0_attn_in['Wo'], 'L0_attn_bo': _L0_attn_in['bo'], 'L0_ffn_Wg': _L0_ffn_in['Wg'], 'L0_ffn_bg': _L0_ffn_in['bg'], 'L0_ffn_W1': _L0_ffn_in['W1'], 'L0_ffn_b1': _L0_ffn_in['b1'], 'L0_ffn_W2': _L0_ffn_in['W2'], 'L0_ffn_b2': _L0_ffn_in['b2'], 'L0_ffn_Wv': _L0_ffn_in['Wv'], 'L0_ffn_bv': _L0_ffn_in['bv'], 'L0_ffn_Wm': _L0_ffn_in['Wm'], 'L0_ffn_bm': _L0_ffn_in['bm'], 'L0_ffn_Wo': _L0_ffn_in['Wo'], 'L0_ffn_bo': _L0_ffn_in['bo'], 'L0_ffn_bk_scale': _L0_ffn_in['bk_scale']}

def reference(x, mask_BS_i2_0, L0_tok_token_table, L0_tok_segm_table, L0_attn_Wq, L0_attn_bq, L0_attn_Wk, L0_attn_bk, L0_attn_Wv, L0_attn_bv, L0_attn_Wo, L0_attn_bo, L0_ffn_Wg, L0_ffn_bg, L0_ffn_W1, L0_ffn_b1, L0_ffn_W2, L0_ffn_b2, L0_ffn_Wv, L0_ffn_bv, L0_ffn_Wm, L0_ffn_bm, L0_ffn_Wo, L0_ffn_bo, L0_ffn_bk_scale):
    import jax
    import jax.numpy as jnp

    def _L0_tok_ref(input_tensor, segment_label, token_table, segm_table):
        import jax, jax.numpy as jnp
        import numpy as np
        VOCAB = 8000
        DIM = 192
        BATCH = 8
        SEQ = 512

        def _sinusoidal_pos(seq_len, dim):
            pos = jnp.arange(seq_len, dtype=jnp.float32)[:, None]
            ids = jnp.arange(dim, dtype=jnp.float32)[None, :]
            even_exp = jnp.floor(ids / 2.0) * 2.0 / dim
            angle = pos / jnp.power(10000.0, even_exp)
            return jnp.where(jnp.arange(dim) % 2 == 0, jnp.sin(angle), jnp.cos(angle))
        batch, seq = input_tensor.shape
        pos = _sinusoidal_pos(seq, token_table.shape[1])
        tokens_embed = token_table[input_tensor]
        segments_embed = segm_table[segment_label]
        return segments_embed + pos[None, :, :] + tokens_embed

    def _L0_attn_ref(X, Wq, bq, Wk, bk, Wv, bv, Wo, bo):
        import jax, jax.numpy as jnp
        import numpy as np
        ROPE_THETA = 10000.0

        def rope(x):
            B, S, D = x.shape
            half = D // 2
            inv_freq = 1.0 / ROPE_THETA ** (jnp.arange(half, dtype=jnp.float32) * 2.0 / D)
            ang = jnp.arange(S, dtype=jnp.float32)[:, None] * inv_freq[None, :]
            cos, sin = (jnp.cos(ang), jnp.sin(ang))
            x1, x2 = (x[..., 0::2], x[..., 1::2])
            r1 = x1 * cos - x2 * sin
            r2 = x1 * sin + x2 * cos
            return jnp.stack([r1, r2], axis=-1).reshape(B, S, D)
        NUM_HEADS = 12
        B, S, D = X.shape
        hd = D // NUM_HEADS
        q = rope(X @ Wq + bq)
        k = rope(X @ Wk + bk)
        v = X @ Wv + bv
        qh = q.reshape(B, S, NUM_HEADS, hd)
        kh = k.reshape(B, S, NUM_HEADS, hd)
        vh = v.reshape(B, S, NUM_HEADS, hd)
        scores = jnp.einsum('bqhd,bkhd->bhqk', qh, kh) / jnp.sqrt(jnp.float32(hd))
        causal = jnp.tril(jnp.ones((S, S), dtype=bool))
        scores = jnp.where(causal[None, None, :, :], scores, -jnp.inf)
        weights = jax.nn.softmax(scores, axis=-1)
        out = jnp.einsum('bhqk,bkhd->bqhd', weights, vh).reshape(B, S, D)
        return out @ Wo + bo

    def _L0_ffn_ref(x, Wg, bg, W1, b1, W2, b2, Wv, bv, Wm, bm, Wo, bo, bk_scale):
        import jax, jax.numpy as jnp
        import numpy as np
        B, N, D, E = (2, 512, 192, 8)
        H = 4 * D
        TARGET_SPARSITY = 0.6
        K_KEEP = int(N * (1.0 - TARGET_SPARSITY))
        V_MAX, FEAT_CLAMP, ETA = (3.0, 10.0, 1.0)

        def _bk_gii(v):
            dr, di = (v, jnp.full_like(v, -ETA))

            def cf(reverse):
                init = (jnp.full((v.shape[0],), 1e+18, v.dtype), jnp.zeros((v.shape[0],), v.dtype))

                def step(c, d):
                    ar, ai = c
                    drr, dii = d
                    den = ar * ar + ai * ai
                    out = (drr - ar / den, dii + ai / den)
                    return (out, out)
                _, (r, i) = jax.lax.scan(step, init, (dr.T, di.T), reverse=reverse)
                return (r.T, i.T)
            ar, ai = cf(False)
            br, bi = cf(True)
            cr, ci = (ar + br - dr, ai + bi - di)
            den = cr * cr + ci * ci
            return (cr / den, -ci / den)
        probs = jax.nn.softmax(x @ Wg + bg, axis=-1)
        top_p = jnp.max(probs, axis=-1)
        comb = jax.nn.one_hot(jnp.argmax(probs, -1), E, dtype=x.dtype) * top_p[..., None]
        h = jax.nn.gelu(jnp.einsum('bnd,edh->ebnh', x, W1) + b1[:, None, None, :])
        y = jnp.einsum('ebnh,ehd->ebnd', h, W2) + b2[:, None, None, :]
        ffn_out = jnp.einsum('ebnd,bne->bnd', y, comb)
        v = jnp.clip(ffn_out @ Wv + bv, -V_MAX, V_MAX)
        scores = jax.nn.sigmoid(x @ Wm + bm)
        thr = jax.lax.top_k(scores, K_KEEP)[0][:, -1]
        mask = (scores >= thr[:, None]).astype(x.dtype)
        gr, gi = _bk_gii(v)
        feats = jnp.clip(jnp.stack([gr, gi], -1) * mask[..., None], -FEAT_CLAMP, FEAT_CLAMP)
        return ffn_out + bk_scale * (feats @ Wo + bo)
    h = _L0_tok_ref(x, mask_BS_i2_0, L0_tok_token_table, L0_tok_segm_table)
    h = h + _L0_attn_ref(_layernorm(h, axis=-1), L0_attn_Wq, L0_attn_bq, L0_attn_Wk, L0_attn_bk, L0_attn_Wv, L0_attn_bv, L0_attn_Wo, L0_attn_bo)
    h = h + _L0_ffn_ref(_layernorm(h, axis=-1), L0_ffn_Wg, L0_ffn_bg, L0_ffn_W1, L0_ffn_b1, L0_ffn_W2, L0_ffn_b2, L0_ffn_Wv, L0_ffn_bv, L0_ffn_Wm, L0_ffn_bm, L0_ffn_Wo, L0_ffn_bo, L0_ffn_bk_scale)
    return h

_drawn_inputs = setup_inputs


def setup_inputs(seed=0):
    import zlib

    import numpy as np

    out = dict(_drawn_inputs(seed))
    spreads = {'L0_attn_bq': (0.0, 0.8),
     'L0_attn_bk': (0.0, 0.8),
     'L0_attn_bv': (0.0, 0.1),
     'L0_attn_bo': (0.0, 0.1),
     'L0_ffn_bg': (0.0, 0.484),
     'L0_ffn_b1': (0.0, 0.8),
     'L0_ffn_b2': (0.0, 0.318),
     'L0_ffn_bo': (0.0, 0.1)}
    factors = {'L0_attn_Wq': 8.0,
     'L0_attn_Wk': 8.0,
     'L0_ffn_W1': 2.754,
     'L0_ffn_Wv': 200.0,
     'L0_ffn_Wm': 8.0,
     'L0_ffn_Wo': 8.0}
    for name, (base, spread) in spreads.items():
        noise = np.random.default_rng([zlib.crc32(name.encode()), seed]).standard_normal(out[name].shape)
        drawn = base * np.exp(spread * noise) if base else spread * noise
        out[name] = jnp.asarray(drawn.astype(out[name].dtype))
    for name, factor in factors.items():
        out[name] = (out[name] * factor).astype(out[name].dtype)
    return out
```

```python
import concourse.bass as bass
from concourse import mybir
from contextlib import ExitStack

fp32 = mybir.dt.float32
fp16 = mybir.dt.float16
bf16 = mybir.dt.bfloat16
i32 = mybir.dt.int32
ALU = mybir.AluOpType
ACT = mybir.ActivationFunctionType
AX = mybir.AxisListType

P = 128
B, S = 2, 2048
N = B * S
D = 192
D1 = D - P
NT = N // P
TB = S // P
QUAD = 4
NQ = NT // QUAD
HEADS, HD = 12, 16
GH = 4
G = HEADS // GH
GD = GH * HD
CH = 512
NCH = S // CH
CT = CH // P
KROWS = 3 * HD
VOCAB, SEGS = 8000, 3
E, HID = 8, 768
HC = HID // P
EPS = 1e-5
KEEP = int(512 * (1.0 - 0.6))
V_MAX, FEAT_CLAMP = 3.0, 10.0
NEG = -1e30
SLOTS = NT + E


START = 1


class Count:

    def __init__(self, sem, base=0):
        self.sem, self.base, self.n = sem, base, 0

    def on(self, instruction, by=1):
        instruction.then_inc(self.sem, by)
        self.n += by
        return self.base + self.n

    def chain(self, engine, instruction):
        engine.wait_ge(self.sem, self.on(instruction))


def hold(engine, sem, value, held):
    engine.wait_ge(sem, value)
    engine.sem_inc(held, 1)


def embed_and_project_values(nc, io, mem, new_sem):
    H, XT0, XT1, VALL, POS, PSB = mem["H"], mem["XT0"], mem["XT1"], mem["VALL"], mem["AO"], mem["PSB"]
    ident = mem["ident"]
    with ExitStack() as c:
        def sb(name, shape, dt=fp32):
            return c.enter_context(nc.sbuf_tensor(name, shape, dt))

        raw = sb("raw_ids", [NT, 2, P], i32)
        rawf = sb("raw_ids_f", [NT, 2, P])
        wrap = sb("wrap", [NT, P])
        tok_f = sb("tok_f", [P, NT])
        tok_i = sb("tok_i", [P, NT], i32)
        lab_f = sb("lab_f", [P, NT])
        one_hot = sb("label_one_hot", [P, SEGS, NT])
        seg_rows = sb("seg_rows", [P, SEGS, D])
        wv0 = sb("wv0", [P, D])
        wv1 = sb("wv1", [D1 + 1, D])
        stats = sb("ln1_stats", [P, QUAD, 6])
        mv = sb("ln1_mean_var", [P, QUAD, 2])
        var_eps = sb("ln1_var_eps", [P, QUAD])
        rstd = sb("ln1_rstd", [P, QUAD])
        minus_half = mem["minus_half"]
        xn = sb("ln1_out", [P, QUAD, D])
        xq0 = sb("xq0", [P, QUAD * P])
        xq1 = sb("xq1", [D1 + 1, QUAD * P])
        zero = sb("zero_rows", [P, 2 * D])

        ids_in, tab_in, zeroed = new_sem("ids_in"), new_sem("tab_in"), new_sem("zeroed")
        zero_ready, ones_rows, pool_done = new_sem("zero_ready"), new_sem("ones_rows_ready"), new_sem("pool1_done")
        held, act_held = new_sem("dve1_held"), new_sem("act1_held")
        ids_t, ids_ready = new_sem("ids_transposed"), new_sem("ids_ready")
        gathered, rows_ready = new_sem("gathered"), new_sem("rows_ready")
        dve_done = new_sem("dve1_done")
        var_ready, rstd_ready = new_sem("var1_ready"), new_sem("rstd1_ready")
        xn_ready, xt_full, xt_free = new_sem("xn1_ready"), new_sem("xt1_full"), new_sem("xt1_free")
        xq_ready, xt_kept = new_sem("xq_ready"), new_sem("xt1_kept")
        v_full, v_kept = new_sem("v_full"), new_sem("v_kept")
        t0 = PSB[:, 0, :]
        t1 = PSB[:, 1, :]
        vp = PSB[:, 2:4, :].rearrange("p a (k n) -> p (a k) n", k=2)

        with nc.Block() as block:
            @block.sync
            def _(sp):
                sp.dma_start(raw[:, 0, :], io["x"].rearrange("b (t p) -> (b t) p", p=P)).then_inc(ids_in, 16)
                sp.dma_start(raw[:, 1, :], io["seg"].rearrange("b (t p) -> (b t) p", p=P)).then_inc(ids_in, 16)
                sp.dma_start(seg_rows[:, :, :].rearrange("p s d -> p (s d)"),
                             io["segm"].rearrange("s d -> (s d)").rearrange("(o n) -> o n", o=1)
                             .broadcast_to([P, SEGS * D])).then_inc(tab_in, 16)
                sp.dma_start(POS[:, 0:TB, :], io["pos"]).then_inc(tab_in, 16)
                sp.dma_start(wv0[:, :], io["Wv"][0:P, :]).then_inc(tab_in, 16)
                sp.dma_start(wv1[0:D1, :], io["Wv"][P:D, :]).then_inc(tab_in, 16)
                sp.dma_start(wv1[D1:D1 + 1, :], io["bv"].rearrange("(o n) -> o n", o=1)).then_inc(tab_in, 16)
                sp.wait_ge(zero_ready, 1)
                slots = io["sorted_x"].rearrange("(a p two) d -> a p (two d)", p=P, two=2)
                for a in range(SLOTS // 2):
                    sp.dma_start(slots[a], zero[:, :]).then_inc(zeroed, 16)
                sp.wait_ge(zeroed, 16 * (SLOTS // 2))

            @block.gpsimd
            def _(pool):
                k = Count(pool_done)
                pool.memset(zero[:, :], 0.0).then_inc(zero_ready, 1)
                k.chain(pool, pool.memset(ident[:, :], 0.0))
                k.chain(pool, pool.affine_select(out=ident[:, :], in_=ident[:, :], compare_op=ALU.not_equal,
                                                 fill=1.0, base=0, pattern=[[-1, P]], channel_multiplier=1))
                k.chain(pool, pool.tensor_copy(mem["ident16"][:, :], ident[:, :]))
                k.chain(pool, pool.tensor_copy(mem["identb"][:, :], ident[:, :]))
                k.chain(pool, pool.memset(mem["masks"][:, :, :], 0.0))
                k.chain(pool, pool.affine_select(out=mem["masks"][:, 0, :], in_=mem["masks"][:, 0, :],
                                                 compare_op=ALU.is_ge, fill=NEG, base=0,
                                                 pattern=[[-1, P]], channel_multiplier=1))
                k.chain(pool, pool.affine_select(out=mem["masks"][:, 1, :], in_=mem["masks"][:, 1, :],
                                                 compare_op=ALU.is_ge, fill=NEG, base=0,
                                                 pattern=[[1, P]], channel_multiplier=-1))
                k.chain(pool, pool.memset(minus_half[:, :], -0.5))
                k.chain(pool, pool.memset(mem["before"][:, :], 1.0))
                k.chain(pool, pool.affine_select(out=mem["before"][:, :], in_=mem["before"][:, :],
                                                 compare_op=ALU.is_gt, fill=0.0, base=0,
                                                 pattern=[[1, P]], channel_multiplier=-1))
                k.chain(pool, pool.memset(mem["ones"][:, :], 1.0))
                pool.wait_ge(ids_ready, 1)
                for q in range(NQ):
                    for t in range(QUAD * q, QUAD * q + QUAD):
                        pool.indirect_dma_start(H[:, t, :], None, io["tok"][:, :],
                                                bass.IndirectOffsetOnAxis(tok_i[:, t:t + 1], 0)).then_inc(gathered, 16)
                    pool.wait_ge(gathered, 16 * QUAD * (q + 1))
                    pool.sem_inc(rows_ready, 1)
                with pool.Fori(0, NQ) as q:
                    pool.wait_ge(var_ready, q + 1)
                    pool.tensor_tensor(rstd[:, :], var_eps[:, :], minus_half[:, 0:QUAD], ALU.pow).then_inc(rstd_ready, 1)

            @block.vector
            def _(dve):
                k = Count(dve_done)
                dve.memset(XT1[D1:D1 + 1, :], 1.0).then_inc(ones_rows, 1)
                dve.memset(xq1[D1:D1 + 1, :], 1.0).then_inc(ones_rows, 1)
                dve.wait_ge(ids_in, 32)
                k.chain(dve, dve.tensor_copy(rawf[:, :, :], raw[:, :, :]))
                for n, rows in ((0, VOCAB), (1, SEGS)):
                    k.chain(dve, dve.tensor_scalar(wrap[:, :], rawf[:, n, :], 0.0, float(rows), ALU.is_lt, ALU.mult))
                    k.chain(dve, dve.tensor_tensor(rawf[:, n, :], rawf[:, n, :], wrap[:, :], ALU.add))
                    k.chain(dve, dve.tensor_scalar(rawf[:, n, :], rawf[:, n, :], 0.0, float(rows - 1), ALU.max, ALU.min))
                dve.wait_ge(ids_t, 1)
                k.chain(dve, dve.tensor_copy(tok_f[:, :], t0[:, 0:NT]))
                dve.tensor_copy(tok_i[:, :], tok_f[:, :]).then_inc(ids_ready, 1)
                k.chain(dve, dve.tensor_copy(lab_f[:, :], t0[:, NT:2 * NT]))
                for s in range(SEGS):
                    k.chain(dve, dve.tensor_scalar(one_hot[:, s, :], lab_f[:, :], float(s), None, ALU.is_equal))
                dve.wait_ge(tab_in, 80)
                dve.sem_inc(xq_ready, START)
                before = k.n
                with dve.Fori(0, B) as b, dve.Fori(0, NQ // B) as r:
                    q = b * (NQ // B) + r
                    k = Count(dve_done, before + q * DVE1)
                    dve.wait_ge(rows_ready, q + 1)
                    h = H[:, bass.ds(q * QUAD, QUAD), :]
                    k.chain(dve, dve.tensor_tensor(h, h, POS[:, bass.ds(r * QUAD, QUAD), :], ALU.add))
                    for s in range(SEGS):
                        for t in range(QUAD):
                            ht = H[:, bass.ds(q * QUAD + t, 1), :].rearrange("p o d -> p (o d)")
                            last = k.on(dve.scalar_tensor_tensor(
                                out=ht, in0=seg_rows[:, s, :], scalar=one_hot[:, s, bass.ds(q * QUAD + t, 1)],
                                in1=ht, op0=ALU.mult, op1=ALU.add))
                        hold(dve, dve_done, last, held)
                    for t in range(QUAD):
                        last = k.on(dve.bn_stats(stats[:, t, :], H[:, bass.ds(q * QUAD + t, 1), :].rearrange("p o d -> p (o d)")))
                    hold(dve, dve_done, last, held)
                    for t in range(QUAD):
                        last = k.on(dve.bn_aggr(mv[:, t, :], stats[:, t, :]))
                    dve.wait_ge(dve_done, last)
                    dve.tensor_scalar(var_eps[:, :], mv[:, :, 1], EPS, None, ALU.add).then_inc(var_ready, 1)
                    dve.wait_ge(rstd_ready, q + 1)
                    for t in range(QUAD):
                        k.on(dve.tensor_scalar(xn[:, t, :], H[:, bass.ds(q * QUAD + t, 1), :].rearrange("p o d -> p (o d)"),
                                               mv[:, t, 0:1], rstd[:, t:t + 1], ALU.subtract, ALU.mult))
                    assert k.n == DVE1, k.n
                    dve.wait_ge(xt_full, q + 1)
                    dve.wait_ge(xt_kept, q + START)
                    dve.wait_ge(v_full, q + START)
                    dve.tensor_scalar(xq0[:, :], t0, 1.0, None, ALU.mult).then_inc(xq_ready, 1)
                    dve.tensor_scalar(xq1[0:D1, :], t1[0:D1, :], 1.0, None, ALU.mult).then_inc(xq_ready, 1)

            @block.tensor
            def _(pe):
                pe.wait_ge(ones_rows, 2)
                pe.wait_ge(pool_done, POOL1)
                pe.wait_ge(dve_done, 7)
                pe.transpose(t0[:, 0:NT], rawf[:, 0, :], ident[0:NT, 0:NT])
                pe.transpose(t0[:, NT:2 * NT], rawf[:, 1, :], ident[0:NT, 0:NT]).then_inc(ids_t, 1)
                pe.wait_ge(tab_in, 80)
                pe.sem_inc(v_full, START)
                with pe.Fori(0, NQ) as q:
                    pe.wait_ge(xq_ready, 2 * q + START)
                    pe.wait_ge(dve_done, DVE1_HEAD + (q + 1) * DVE1)
                    for t in range(QUAD):
                        pe.transpose(t0[:, t * P:(t + 1) * P], xn[:, t, 0:P], ident[:, :])
                    for t in range(QUAD):
                        last = pe.transpose(t1[0:D1, t * P:(t + 1) * P], xn[:, t, P:D], ident[:, :])
                    last.then_inc(xt_full, 1)
                    pe.wait_ge(v_kept, q + START)
                    pe.wait_ge(xq_ready, 2 * q + 2 + START)
                    for t in range(QUAD):
                        pe.matmul(vp[:, t, 0:D], xq0[:, t * P:(t + 1) * P], wv0[:, :], start=True, stop=False)
                        last = pe.matmul(vp[:, t, 0:D], xq1[:, t * P:(t + 1) * P], wv1[:, :], start=False, stop=True)
                    last.then_inc(v_full, 1)

            @block.scalar
            def _(act):
                act.sem_inc(xt_kept, START)
                act.sem_inc(v_kept, START)
                with act.Fori(0, NQ) as q:
                    hold(act, xq_ready, 2 * q + 2 + START, act_held)
                    act.activation(XT0[:, bass.ds(q * QUAD * P, QUAD * P)], xq0[:, :], ACT.Copy)
                    act.activation(XT1[0:D1, bass.ds(q * QUAD * P, QUAD * P)], xq1[0:D1, :], ACT.Copy).then_inc(xt_kept, 1)
                    hold(act, v_full, q + 1 + START, act_held)
                    act.activation(VALL[:, bass.ds(q * QUAD, QUAD), :], vp[:, :, 0:D], ACT.Copy).then_inc(v_kept, 1)


POOL1 = 10
DVE1 = 1 + SEGS * QUAD + 3 * QUAD
DVE1_HEAD = 12


def attention_order():
    order = [("project", 0, 0)] + [("max", 0, n) for n in range(PIECES[0])] + [("shift", 0, 0)]
    for c in range(NCH):
        steps = CT * (c + 1)
        between = [("norm", c - 1, 0)] if c else []
        if c + 1 < NCH:
            between += [("project", c + 1, 0)]
        pieces = [("max", c + 1, n) for n in range(PIECES[c + 1])] if c + 1 < NCH else []
        sent = 0
        for j in range(steps):
            order.append(("scores", c, j))
            if j == 0:
                order += between
            else:
                upto = len(pieces) * j // max(steps - 2, 1)
                order += pieces[sent:upto]
                if pieces and sent < len(pieces) <= upto:
                    order.append(("shift", c + 1, 0))
                sent = max(sent, min(upto, len(pieces)))
                order.append(("values", c, j - 1))
        order.append(("values", c, steps - 1))
    return order + [("norm", NCH - 1, 0)]


PIECES = [CT * GH * (c + 1) for c in range(NCH)]
ALL_PIECES = sum(PIECES)
STEPS = [CT * (c + 1) for c in range(NCH)]
ALL_STEPS = sum(STEPS)
MISC = 3 * NCH
STACKS = 3 * 2 * GH
SHIFT_ROWS = 16 * 2 * GH
ORDER = attention_order()
MISC_USE = {key: n for n, key in enumerate([(what, c) for what, c, _ in ORDER if what in ("project", "shift", "norm")])}


def piece(c, n):
    return n // (GH * (c + 1)), n // (c + 1) % GH, n % (c + 1)


def width(c, qt, kc):
    return (qt + 1) * P if kc == c else CH


def first_query(c, j):
    return max(0, j - CT * c) * P


def attention(nc, io, mem, new_sem):
    XT0, XT1, VALL, AO, PSB = mem["XT0"], mem["XT1"], mem["VALL"], mem["AO"], mem["PSB"]
    with ExitStack() as ctx:
        def sb(name, shape, dt=fp32):
            return ctx.enter_context(nc.sbuf_tensor(name, shape, dt))

        wq0 = sb("wqk0", [P, 2, GD])
        wq1 = sb("wqk1", [D1 + 1, 2, GD])
        rope = sb("rope", [P, 2, 2, CH])
        xc = sb("x_cos", [P, CH])
        sh = sb("x_turned", [P, CH])
        ss = sb("x_sin", [P, CH])
        rot = sb("rotated", [P, CH])
        hi = sb("rot_high", [P, CH], fp16)
        lo = sb("rot_low", [P, CH], fp16)
        QT = sb("QT", [P // 2, GH, S], fp16)
        KT = sb("KT", [P // 2, GH, S], fp16)
        VG = sb("VG", [P, TB, GH, 32])
        probs = sb("probs", [P, 2, GH, CH])
        tops = sb("piece_max", [P, CT * GH, NCH])
        top = sb("row_max", [P, CT * GH])
        shift = sb("shift", [P, 2, CT * GH], fp16)
        shiftT = sb("shiftT", [2 * CT * GH, P], fp16)
        OT = sb("OT", [P, CH])
        rcp = sb("row_rcp", [P, CT, GH])

        w_in, stack, mrow = new_sem("wqk_in"), new_sem("stack_in"), new_sem("shift_rows_in")
        rope_in = [new_sem("rope_in0"), new_sem("rope_in1")]
        misc_full, misc_free = new_sem("misc_full"), new_sem("misc_free")
        max_full, max_free = new_sem("piece_full"), new_sem("piece_free")
        s_full, p_full, pv_done = new_sem("scores_full"), new_sem("probs_ready"), new_sem("values_done")
        ot_full, turned, split = new_sem("ot_full"), new_sem("turned"), new_sem("split_ready")
        rot_done, shift_ready, vg_ready = new_sem("pool2_done"), new_sem("shift_ready"), new_sem("vg_ready")
        dve_done, const2, const2p = new_sem("dve2_done"), new_sem("const2_dve"), new_sem("const2_pool")
        held, sp_held = new_sem("dve2_held"), new_sem("sp2_held")

        def sbank(pr):
            return PSB[:, 2 * pr:2 * pr + 2, :]

        obank = PSB[:, 6, :]
        misc = PSB[:, 7, :]
        with nc.Block() as block:
            @block.sync
            def _(sp):
                with sp.Fori(0, B) as b, sp.Fori(0, G) as g:
                    it = b * G + g
                    for n, w in enumerate(("q", "k")):
                        sp.dma_start(wq0[:, n, :], io["W" + w][0:P, bass.ds(g * GD, GD)]).then_inc(w_in, 16)
                        sp.dma_start(wq1[0:D1, n, :], io["W" + w][P:D, bass.ds(g * GD, GD)]).then_inc(w_in, 16)
                        sp.dma_start(wq1[D1:D1 + 1, n, :], io["b" + w][bass.ds(g * GD, GD)].rearrange("(o n) -> o n", o=1)).then_inc(w_in, 16)
                    for c in range(2):
                        sp.dma_start(rope[:, c, :, :], io["rope"][bass.ds(g * NCH + c, 1), :, :, :].rearrange("o p a n -> (o p) a n")).then_inc(rope_in[c], 16)
                    for c in range(NCH):
                        if c >= 2:
                            sp.wait_ge(rot_done, it * (4 * NCH) + 4 * (c - 1))
                            sp.dma_start(rope[:, c % 2, :, :], io["rope"][bass.ds(g * NCH + c, 1), :, :, :].rearrange("o p a n -> (o p) a n")).then_inc(rope_in[c % 2], 16)
                        sp.wait_ge(rot_done, it * (4 * NCH) + 4 * (c + 1))
                        cols = slice(c * CH, (c + 1) * CH)
                        for dst, first, parts in ((QT, 0, (hi, hi, lo)), (KT, GD, (hi, lo, hi))):
                            for h in range(GH):
                                for n, part in enumerate(parts):
                                    sp.dma_start(dst[n * HD:(n + 1) * HD, h, cols],
                                                 part[first + h * HD:first + (h + 1) * HD, :]).then_inc(stack, 16)
                        hold(sp, stack, (it * NCH + c + 1) * (16 * STACKS), sp_held)
                        sp.wait_ge(misc_free, it * MISC + MISC_USE["shift", c] + 1 + START)
                        for n in range(2):
                            for h in range(GH):
                                row = (n * GH + h) * CT
                                sp.dma_start(QT[KROWS + n:KROWS + n + 1, h, cols].rearrange("o (t q) -> o t q", q=P),
                                             shiftT[row:row + CT, :]).then_inc(mrow, 16)

            @block.gpsimd
            def _(pool):
                pool.memset(KT[32:64, :, :], 1.0).then_inc(const2p, 1)
                pool.wait_ge(const2p, 1)
                with pool.Fori(0, B * G) as it:
                    for c in range(NCH):
                        k = Count(rot_done, it * (4 * NCH) + 4 * c)
                        pool.wait_ge(turned, it * NCH + c + 1)
                        k.chain(pool, pool.tensor_tensor(ss[:, :], sh[:, :], rope[:, c % 2, 1, :], ALU.mult))
                        k.on(pool.tensor_tensor(rot[:, :], xc[:, :], ss[:, :], ALU.add))
                        if c:
                            pool.wait_ge(stack, (it * NCH + c) * (16 * STACKS))
                        k.chain(pool, pool.tensor_tensor(hi[:, :], xc[:, :], ss[:, :], ALU.add))
                        k.chain(pool, pool.tensor_tensor(lo[:, :], rot[:, :], hi[:, :], ALU.subtract))

            @block.tensor
            def _(pe):
                with pe.Fori(0, B) as b, pe.Fori(0, G) as g:
                    it = b * G + g
                    pieces = step = 0
                    for what, c, n in ORDER:
                        if (what, c) in MISC_USE:
                            pe.wait_ge(misc_free, it * MISC + MISC_USE[what, c] + START)
                        if what == "project":
                            if c == 0:
                                pe.wait_ge(w_in, (it + 1) * 96)
                            at = b * S + c * CH
                            pe.matmul(misc, wq0[:, :, :].rearrange("p a n -> p (a n)"), XT0[:, bass.ds(at, CH)], start=True, stop=False)
                            pe.matmul(misc, wq1[:, :, :].rearrange("p a n -> p (a n)"), XT1[:, bass.ds(at, CH)], start=False, stop=True).then_inc(misc_full, 1)
                        elif what == "max":
                            if n == 0:
                                pe.wait_ge(stack, (it * NCH + c + 1) * (16 * STACKS))
                            pe.wait_ge(max_free, it * ALL_PIECES + max(pieces - 1, 0) + START)
                            qt, h, kc = piece(c, n)
                            w, at = width(c, qt, kc), (c * CT + qt) * P
                            bank = PSB[:, 4 + pieces % 2, :]
                            mm = pe.matmul(bank[:, 0:w], QT[0:KROWS, h, at:at + P], KT[0:KROWS, h, kc * CH:kc * CH + w],
                                           start=True, stop=kc != c)
                            if kc == c:
                                mm = pe.matmul(bank[:, w - P:w], mem["identb"][:, :], mem["masks"][:, 0, :], start=False, stop=True)
                            mm.then_inc(max_full, 1)
                            pieces += 1
                        elif what == "shift":
                            pe.wait_ge(shift_ready, it * NCH + c + 1)
                            pe.transpose(misc.bitcast(fp16)[0:2 * CT * GH, 0:P], shift[:, :, :].rearrange("p a n -> p (a n)"),
                                         mem["ident16"][:, :]).then_inc(misc_full, 1)
                        elif what == "scores":
                            q0 = first_query(c, n)
                            if n == 0:
                                pe.wait_ge(mrow, (it * NCH + c + 1) * SHIFT_ROWS)
                            for pr in range(2):
                                if step:
                                    pe.wait_ge(p_full, it * (2 * ALL_STEPS) + 2 * step - 1 + pr)
                                for h in (2 * pr, 2 * pr + 1):
                                    dst = sbank(pr)[:, h % 2, q0:CH]
                                    mm = pe.matmul(dst, KT[0:KROWS + 2, h, n * P:(n + 1) * P], QT[0:KROWS + 2, h, c * CH + q0:(c + 1) * CH],
                                                   start=True, stop=n < CT * c)
                                    if n >= CT * c:
                                        mm = pe.matmul(dst[:, 0:P], mem["identb"][:, :], mem["masks"][:, 1, :], start=False, stop=True)
                                mm.then_inc(s_full, 1)
                            step += 1
                        elif what == "values":
                            q0 = first_query(c, n)
                            at = sum(STEPS[:c]) + n
                            pe.wait_ge(p_full, it * (2 * ALL_STEPS) + 2 * at + 2)
                            if n == 0:
                                if c:
                                    pe.wait_ge(ot_full, it * NCH + c)
                                else:
                                    pe.wait_ge(vg_ready, it + 1)
                            for h in range(GH):
                                mm = pe.matmul(obank[32 * h:32 * h + 32, q0:CH], VG[:, n, h, :], probs[:, at % 2, h, q0:CH],
                                               start=n == 0, stop=n == STEPS[c] - 1)
                            mm.then_inc(pv_done, 1)
                        elif what == "norm":
                            pe.wait_ge(ot_full, it * NCH + c + 1)
                            for t in range(CT):
                                mm = pe.transpose(misc[:, t * P:(t + 1) * P], OT[:, t * P:(t + 1) * P], mem["ident"][:, :])
                            mm.then_inc(misc_full, 1)

            @block.scalar
            def _(act):
                with act.Fori(0, B * G) as it:
                    step = 0
                    for what, c, n in ORDER:
                        if what == "scores":
                            q0 = first_query(c, n)
                            if step >= 2:
                                act.wait_ge(pv_done, it * ALL_STEPS + step - 1)
                            for pr in range(2):
                                act.wait_ge(s_full, it * (2 * ALL_STEPS) + 2 * step + pr + 1)
                                act.activation(probs[:, step % 2, 2 * pr:2 * pr + 2, q0:CH], sbank(pr)[:, :, q0:CH], ACT.Exp,
                                               scale=1.0 / HD ** 0.5).then_inc(p_full, 1)
                            step += 1
                        elif what == "values" and n == STEPS[c] - 1:
                            act.wait_ge(pv_done, it * ALL_STEPS + sum(STEPS[:c + 1]))
                            if c:
                                act.wait_ge(misc_full, it * MISC + MISC_USE["norm", c - 1] + 1)
                            act.activation(OT[:, :], obank, ACT.Copy).then_inc(ot_full, 1)

            @block.vector
            def _(dve):
                dve.memset(VG[:, :, :, HD:32], 0.0).then_inc(const2, 1)
                dve.wait_ge(const2, 1)
                dve.memset(VG[:, :, :, HD:HD + 1], 1.0).then_inc(const2, 1)
                dve.sem_inc(misc_free, START)
                dve.sem_inc(max_free, START)
                with dve.Fori(0, B) as b, dve.Fori(0, G) as g:
                    it = b * G + g
                    k = Count(dve_done, it * DVE2)
                    pieces = 0
                    dve.tensor_scalar(VG[:, :, :, 0:HD], VALL[:, bass.ds(b * TB, TB), bass.ds(g * GD, GD)].rearrange("p t (h d) -> p t h d", d=HD),
                                      1.0, None, ALU.mult).then_inc(vg_ready, 1)
                    for what, c, n in ORDER:
                        if what == "project":
                            dve.wait_ge(rope_in[c % 2], it * 32 + 16 * (c // 2 + 1))
                            if c:
                                dve.wait_ge(rot_done, it * (4 * NCH) + 4 * c)
                            dve.wait_ge(misc_full, it * MISC + MISC_USE["project", c] + 1)
                            k.on(dve.tensor_tensor(xc[:, :], misc, rope[:, c % 2, 0, :], ALU.mult))
                            dve.stream_shuffle(sh[:, :], misc, [p ^ 1 for p in range(32)]).then_inc(turned, 1)
                            hold(dve, turned, it * NCH + c + 1, held)
                            dve.sem_inc(misc_free, 1)
                        elif what == "max":
                            qt, h, kc = piece(c, n)
                            dve.wait_ge(max_full, it * ALL_PIECES + pieces + 1)
                            dve.tensor_reduce(tops[:, h * CT + qt, kc:kc + 1], PSB[:, 4 + pieces % 2, 0:width(c, qt, kc)], AX.X, ALU.max).then_inc(max_free, 1)
                            pieces += 1
                        elif what == "shift":
                            dve.wait_ge(max_free, it * ALL_PIECES + pieces + START)
                            k.chain(dve, dve.tensor_reduce(top[:, :], tops[:, :, 0:c + 1], AX.X, ALU.max))
                            k.chain(dve, dve.tensor_scalar(shift[:, 0, :], top[:, :], -1.0, None, ALU.mult))
                            dve.scalar_tensor_tensor(out=shift[:, 1, :], in0=top[:, :], scalar=-1.0, in1=shift[:, 0, :],
                                                     op0=ALU.mult, op1=ALU.subtract).then_inc(shift_ready, 1)
                            if c:
                                dve.wait_ge(mrow, (it * NCH + c) * SHIFT_ROWS)
                            dve.wait_ge(misc_full, it * MISC + MISC_USE["shift", c] + 1)
                            dve.tensor_copy(shiftT[:, :], misc.bitcast(fp16)[0:2 * CT * GH, 0:P]).then_inc(misc_free, 1)
                        elif what == "norm":
                            dve.wait_ge(misc_full, it * MISC + MISC_USE["norm", c] + 1)
                            heads = misc.rearrange("p (t h d) -> p t h d", t=CT, h=GH)
                            k.chain(dve, dve.reciprocal(rcp[:, :, :], heads[:, :, :, HD]))
                            dst = AO[:, bass.ds(b * TB + c * CT, CT), bass.ds(g * GD, GD)].rearrange("p t (h d) -> p t h d", d=HD)
                            dve.tensor_tensor(dst, heads[:, :, :, 0:HD], rcp[:, :, :].unsqueeze(3).broadcast_to([P, CT, GH, HD]), ALU.mult).then_inc(misc_free, 1)
                    assert k.n == DVE2, k.n


DVE2 = NCH * 4


GATES = E + 1
DVE3 = 1 + 2 * QUAD


def mix_and_norm(nc, io, mem, new_sem):
    H, AO, XN2, PSB, ident, LG = mem["H"], mem["AO"], mem["VALL"], mem["PSB"], mem["ident"], mem["LG"]
    with ExitStack() as ctx:
        def sb(name, shape, dt=fp32):
            return ctx.enter_context(nc.sbuf_tensor(name, shape, dt))

        wo0, wo1 = sb("wo0", [P, D]), sb("wo1", [D1 + 1, D])
        wg0, wg1 = sb("wg0", [P, GATES]), sb("wg1", [D1 + 1, GATES])
        aq = sb("aq", [P, QUAD, D])
        a0, a1 = sb("a0", [P, QUAD * P]), sb("a1", [D1 + 1, QUAD * P])
        xq = sb("xn2_quad", [P, QUAD, D])
        x0, x1 = sb("x0", [P, QUAD * P]), sb("x1", [D1 + 1, QUAD * P])
        stats, mv = sb("ln2_stats", [P, QUAD, 6]), sb("ln2_mean_var", [P, QUAD, 2])
        var_eps, rstd = sb("ln2_var_eps", [P, QUAD]), sb("ln2_rstd", [P, QUAD])

        w_in, ones_rows = new_sem("wog_in"), new_sem("ones_rows3")
        aq_ready, at_full, a_ready, h_full = new_sem("aq_ready"), new_sem("at_full"), new_sem("a_ready"), new_sem("mix_full")
        dve_done, var_ready, rstd_ready = new_sem("dve3_done"), new_sem("var2_ready"), new_sem("rstd2_ready")
        xq_ready, xq_kept = new_sem("xn2_ready"), new_sem("xn2_kept")
        xt_full, x_ready = new_sem("xt2_full"), new_sem("x2_ready")
        g_full, g_ready, held, act_held = new_sem("gates_full"), new_sem("gates_ready"), new_sem("dve3_held"), new_sem("act3_held")
        at0, at1 = PSB[:, 0, :], PSB[:, 1, :]
        mix = PSB[:, 2:4, :].rearrange("p a (k n) -> p (a k) n", k=2)
        xt0, xt1 = PSB[:, 4, :], PSB[:, 5, :]
        gates = PSB[:, 6, 0:QUAD * 16].rearrange("p (t n) -> p t n", n=16)

        with nc.Block() as block:
            @block.sync
            def _(sp):
                def row(a):
                    return a.rearrange("(o n) -> o n", o=1)
                for dst, src in ((wo0[:, :], io["Wo"][0:P, :]), (wo1[0:D1, :], io["Wo"][P:D, :]),
                                 (wo1[D1:D1 + 1, :], row(io["bo"])),
                                 (wg0[:, 0:E], io["Wg"][0:P, :]), (wg1[0:D1, 0:E], io["Wg"][P:D, :]),
                                 (wg1[D1:D1 + 1, 0:E], row(io["bg"])),
                                 (wg0[:, E:GATES], io["Wm"][0:P].rearrange("(p o) -> p o", o=1)),
                                 (wg1[0:D1, E:GATES], io["Wm"][P:D].rearrange("(p o) -> p o", o=1)),
                                 (wg1[D1:D1 + 1, E:GATES], row(io["bm"]))):
                    sp.dma_start(dst, src).then_inc(w_in, 16)

            @block.gpsimd
            def _(pool):
                with pool.Fori(0, NQ) as q:
                    pool.wait_ge(var_ready, q + 1)
                    pool.tensor_tensor(rstd[:, :], var_eps[:, :], mem["minus_half"][:, 0:QUAD], ALU.pow).then_inc(rstd_ready, 1)

            @block.tensor
            def _(pe):
                pe.wait_ge(w_in, 16 * 9)
                pe.wait_ge(ones_rows, 2)
                pe.sem_inc(xt_full, START)
                with pe.Fori(0, NQ) as q:
                    pe.wait_ge(a_ready, 2 * q + START)
                    pe.wait_ge(aq_ready, q + 1)
                    for t in range(QUAD):
                        pe.transpose(at0[:, t * P:(t + 1) * P], aq[:, t, 0:P], ident[:, :])
                    for t in range(QUAD):
                        last = pe.transpose(at1[0:D1, t * P:(t + 1) * P], aq[:, t, P:D], ident[:, :])
                    last.then_inc(at_full, 1)
                    pe.wait_ge(a_ready, 2 * q + 2 + START)
                    pe.wait_ge(dve_done, q * DVE3 + START)
                    for t in range(QUAD):
                        pe.matmul(mix[:, t, 0:D], a0[:, t * P:(t + 1) * P], wo0[:, :], start=True, stop=False)
                        last = pe.matmul(mix[:, t, 0:D], a1[:, t * P:(t + 1) * P], wo1[:, :], start=False, stop=True)
                    last.then_inc(h_full, 1)
                    pe.wait_ge(xq_ready, QUAD * (q + 1))
                    pe.wait_ge(x_ready, 2 * q + START)
                    for t in range(QUAD):
                        pe.transpose(xt0[:, t * P:(t + 1) * P], xq[:, t, 0:P], ident[:, :])
                    for t in range(QUAD):
                        last = pe.transpose(xt1[0:D1, t * P:(t + 1) * P], xq[:, t, P:D], ident[:, :])
                    last.then_inc(xt_full, 1)
                    pe.wait_ge(x_ready, 2 * q + 2 + START)
                    pe.wait_ge(g_ready, q + START)
                    for t in range(QUAD):
                        pe.matmul(gates[:, t, 0:GATES], x0[:, t * P:(t + 1) * P], wg0[:, :], start=True, stop=False)
                        last = pe.matmul(gates[:, t, 0:GATES], x1[:, t * P:(t + 1) * P], wg1[:, :], start=False, stop=True)
                    last.then_inc(g_full, 1)

            @block.scalar
            def _(act):
                def quad_in(q):
                    act.activation(aq[:, :, :], AO[:, bass.ds(q * QUAD, QUAD), :], ACT.Copy).then_inc(aq_ready, 1)

                def round_of(q, more):
                    act.wait_ge(at_full, q + 1)
                    act.activation(a0[:, :], at0, ACT.Copy).then_inc(a_ready, 1)
                    act.activation(a1[0:D1, :], at1[0:D1, :], ACT.Copy).then_inc(a_ready, 1)
                    if more:
                        quad_in(q + 1)
                    act.wait_ge(xt_full, q + 1 + START)
                    act.activation(x0[:, :], xt0, ACT.Copy).then_inc(x_ready, 1)
                    act.activation(x1[0:D1, :], xt1[0:D1, :], ACT.Copy).then_inc(x_ready, 1)
                    hold(act, xq_ready, QUAD * (q + 1), act_held)
                    act.activation(XN2[:, bass.ds(q * QUAD, QUAD), :], xq[:, :, :], ACT.Copy).then_inc(xq_kept, 1)
                    hold(act, g_full, q + 1, act_held)
                    act.activation(LG[:, bass.ds(q * QUAD, QUAD), :], gates[:, :, 0:GATES], ACT.Copy).then_inc(g_ready, 1)

                for sem in (a_ready, x_ready, g_ready, xq_kept):
                    act.sem_inc(sem, START)
                quad_in(0)
                with act.Fori(0, NQ - 1) as q:
                    round_of(q, True)
                round_of(NQ - 1, False)

            @block.vector
            def _(dve):
                dve.memset(a1[D1:D1 + 1, :], 1.0).then_inc(ones_rows, 1)
                dve.memset(x1[D1:D1 + 1, :], 1.0).then_inc(ones_rows, 1)
                dve.sem_inc(dve_done, START)
                with dve.Fori(0, NQ) as q:
                    k = Count(dve_done, q * DVE3 + START)
                    h = H[:, bass.ds(q * QUAD, QUAD), :]
                    dve.wait_ge(h_full, q + 1)
                    last = k.on(dve.tensor_tensor(h, h, mix[:, :, 0:D], ALU.add))
                    hold(dve, dve_done, last, held)
                    for t in range(QUAD):
                        last = k.on(dve.bn_stats(stats[:, t, :], H[:, bass.ds(q * QUAD + t, 1), :].rearrange("p o d -> p (o d)")))
                    hold(dve, dve_done, last, held)
                    for t in range(QUAD):
                        last = k.on(dve.bn_aggr(mv[:, t, :], stats[:, t, :]))
                    dve.wait_ge(dve_done, last)
                    dve.tensor_scalar(var_eps[:, :], mv[:, :, 1], EPS, None, ALU.add).then_inc(var_ready, 1)
                    dve.wait_ge(xq_kept, q + START)
                    dve.wait_ge(xt_full, q + START)
                    dve.wait_ge(rstd_ready, q + 1)
                    for t in range(QUAD):
                        dve.tensor_scalar(xq[:, t, :], H[:, bass.ds(q * QUAD + t, 1), :].rearrange("p o d -> p (o d)"),
                                          mv[:, t, 0:1], rstd[:, t:t + 1], ALU.subtract, ALU.mult).then_inc(xq_ready, 1)
                    assert k.n == DVE3, k.n


def route(nc, io, mem, new_sem):
    XN2, PSB, ident, LG = mem["VALL"], mem["PSB"], mem["ident"], mem["LG"]
    top_p, score, dest = mem["top_p"], mem["score"], mem["dest"]
    logits, z = LG[:, 0:NT, 0:E], LG[:, 0:NT, E]
    with ExitStack() as ctx:
        def sb(name, shape, dt=fp32):
            return ctx.enter_context(nc.sbuf_tensor(name, shape, dt))

        best, less, ex = sb("best", [P, NT]), sb("below_best", [P, NT, E]), sb("exp_logits", [P, NT, E])
        total, ez = sb("exp_sum", [P, NT]), sb("exp_score", [P, NT])
        eq = sb("is_best", [P, NT, E])
        run = [sb("run_a", [P, NT, E]), sb("run_b", [P, NT, E])]
        oh = sb("expert_one_hot", [P, NT, E])
        tot = [sb("tiles_a", [P, NT, E]), sb("tiles_b", [P, NT, E])]
        own = sb("tile_counts", [P, NT, E])
        whole_i, whole = sb("whole_tiles_i", [P, E], i32), sb("whole_tiles", [P, E])
        end = [sb("end_a", [P, E]), sb("end_b", [P, E])]
        base = sb("expert_base", [P, E])
        place = sb("place", [P, NT, E])
        dest_f = sb("dest_f", [P, NT])
        starts_i, starts = sb("tile_starts_i", [1, SLOTS], i32), sb("tile_starts", [1, SLOTS])
        passed = sb("experts_passed", [1, SLOTS, E])
        expert_f = sb("tile_expert_f", [1, SLOTS])
        sT = sb("score_rows_sb", [NT, P])

        dve_done, pool_done, ex_ready = new_sem("dve4_done"), new_sem("pool4_done"), new_sem("exps_ready")
        less_ready, oh_ready, ranks_full = new_sem("less_ready"), new_sem("one_hot_ready"), new_sem("ranks_full")
        score_ready, sT_full, sT_ready, s_out = new_sem("score_ready"), new_sem("sT_full"), new_sem("sT_ready"), new_sem("score_out")
        dest_ready, scattered, table_ready = new_sem("dest_ready"), new_sem("scattered"), new_sem("table_ready")
        ranks, totals, st = PSB[:, 0, 0:NT * E].rearrange("p (t e) -> p t e", e=E), PSB[:, 1, 0:NT * E].rearrange("p (t e) -> p t e", e=E), PSB[:, 2, 0:P]
        SB = mem["score_all"]

        with nc.Block() as block:
            @block.vector
            def _(dve):
                k = Count(dve_done)
                k.chain(dve, dve.tensor_reduce(best[:, :], logits, AX.X, ALU.max))
                dve.tensor_tensor(less[:, :, :], logits, best[:, :].unsqueeze(2).broadcast_to([P, NT, E]), ALU.subtract).then_inc(less_ready, 1)
                dve.wait_ge(less_ready, 1)
                k.chain(dve, dve.tensor_scalar(eq[:, :, :], less[:, :, :], 0.0, None, ALU.is_equal))
                now = eq
                for n, s in enumerate((1, 2, 4)):
                    new = run[n % 2]
                    k.on(dve.tensor_copy(new[:, :, 0:s], now[:, :, 0:s]))
                    k.chain(dve, dve.tensor_tensor(new[:, :, s:E], now[:, :, s:E], now[:, :, 0:E - s], ALU.add))
                    now = new
                dve.scalar_tensor_tensor(out=oh[:, :, :], in0=now[:, :, :], scalar=1.0, in1=eq[:, :, :],
                                         op0=ALU.is_equal, op1=ALU.mult).then_inc(oh_ready, 1)
                dve.wait_ge(ex_ready, 2)
                k.chain(dve, dve.tensor_scalar(ez[:, :], ez[:, :], 1.0, None, ALU.add))
                dve.reciprocal(score[:, :], ez[:, :]).then_inc(score_ready, 1)
                k.chain(dve, dve.tensor_reduce(total[:, :], ex[:, :, :], AX.X, ALU.add))
                k.chain(dve, dve.reciprocal(top_p[:, :], total[:, :]))
                dve.wait_ge(ranks_full, 1)
                k.chain(dve, dve.tensor_copy(own[:, :, :], totals))
                now = own
                for n in range(5):
                    s, new = 1 << n, tot[n % 2]
                    k.on(dve.tensor_copy(new[:, 0:s, :], now[:, 0:s, :]))
                    k.chain(dve, dve.tensor_tensor(new[:, s:NT, :], now[:, s:NT, :], now[:, 0:NT - s, :], ALU.add))
                    now = new
                k.chain(dve, dve.tensor_tensor(place[:, :, :], now[:, :, :], own[:, :, :], ALU.subtract))
                k.chain(dve, dve.tensor_tensor(place[:, :, :], place[:, :, :], ranks, ALU.add))
                k.chain(dve, dve.tensor_scalar(whole_i[:, :], now[:, NT - 1, :], float(P - 1), None, ALU.add))
                k.chain(dve, dve.tensor_scalar(whole_i[:, :], whole_i[:, :], 7, 7, ALU.logical_shift_right, ALU.logical_shift_left))
                k.chain(dve, dve.tensor_copy(whole[:, :], whole_i[:, :]))
                now = whole
                for n, s in enumerate((1, 2, 4)):
                    new = end[n % 2]
                    k.on(dve.tensor_copy(new[:, 0:s], now[:, 0:s]))
                    k.chain(dve, dve.tensor_tensor(new[:, s:E], now[:, s:E], now[:, 0:E - s], ALU.add))
                    now = new
                ends = now
                k.chain(dve, dve.tensor_tensor(base[:, :], ends[:, :], whole[:, :], ALU.subtract))
                k.chain(dve, dve.tensor_tensor(place[:, :, :], place[:, :, :], base[:, :].unsqueeze(1).broadcast_to([P, NT, E]), ALU.add))
                k.chain(dve, dve.tensor_tensor(place[:, :, :], place[:, :, :], oh[:, :, :], ALU.mult))
                k.chain(dve, dve.tensor_reduce(dest_f[:, :], place[:, :, :], AX.X, ALU.add))
                dve.tensor_copy(dest[:, :], dest_f[:, :]).then_inc(dest_ready, 1)
                dve.wait_ge(pool_done, 1)
                k.chain(dve, dve.tensor_copy(starts[:, :], starts_i[:, :]))
                k.chain(dve, dve.tensor_tensor(passed[:, :, :], ends[0:1, :].unsqueeze(1).broadcast_to([1, SLOTS, E]),
                                               starts[:, :].unsqueeze(2).broadcast_to([1, SLOTS, E]), ALU.is_le))
                k.chain(dve, dve.tensor_reduce(expert_f[:, :], passed[:, :, :], AX.X, ALU.add))
                dve.tensor_scalar(mem["tile_expert"][:, :], expert_f[:, :], float(E - 1), None, ALU.min).then_inc(table_ready, 1)
                dve.wait_ge(sT_full, 1)
                dve.tensor_copy(sT[:, :], st[0:NT, :]).then_inc(sT_ready, 1)

            @block.scalar
            def _(act):
                act.wait_ge(less_ready, 1)
                act.activation(ex[:, :, :], less[:, :, :], ACT.Exp).then_inc(ex_ready, 1)
                act.activation(ez[:, :], z, ACT.Exp, scale=-1.0).then_inc(ex_ready, 1)

            @block.tensor
            def _(pe):
                pe.wait_ge(oh_ready, 1)
                pe.matmul(ranks, mem["before"][:, :], oh[:, :, :], start=True, stop=True)
                pe.matmul(totals, mem["ones"][:, :], oh[:, :, :], start=True, stop=True).then_inc(ranks_full, 1)
                pe.wait_ge(score_ready, 1)
                pe.transpose(st[0:NT, :], score[:, :], ident[:, :]).then_inc(sT_full, 1)

            @block.gpsimd
            def _(pool):
                pool.iota(starts_i[:, :], pattern=[[P, SLOTS]], base=0, channel_multiplier=0).then_inc(pool_done, 1)
                pool.wait_ge(dest_ready, 1)
                for t in range(NT):
                    pool.indirect_dma_start(io["sorted_x"][:, :], bass.IndirectOffsetOnAxis(dest[:, t:t + 1], 0),
                                            XN2[:, t, :], None).then_inc(scattered, 16)
                pool.wait_ge(scattered, 16 * NT)

            @block.sync
            def _(sp):
                sp.wait_ge(sT_ready, 1)
                sp.dma_start(io["score_rows"].rearrange("b (t p) -> (b t) p", p=P), sT[:, :]).then_inc(s_out, 16)
                sp.wait_ge(s_out, 16)
                for b in range(B):
                    sp.dma_start(SB[:, b, :], io["score_rows"][b:b + 1, :].broadcast_to([P, S])).then_inc(s_out, 16)
                sp.wait_ge(s_out, 48)


HROW = HC // 2 * P


def experts(nc, io, mem, new_sem):
    PSB, ident = mem["PSB"], mem["ident"]
    score, rank, SB = mem["score"], mem["rank"], mem["score_all"]
    with ExitStack() as ctx:
        def sb(name, shape, dt=fp32):
            return ctx.enter_context(nc.sbuf_tensor(name, shape, dt))

        w1a, w1b = sb("w1a", [P, 2, HID]), sb("w1b", [D1 + 1, 2, HID])
        w2 = sb("w2", [P, 2, HC, D])
        b2 = sb("b2", [P, 2, D])
        xs = sb("xs", [P, 2, D])
        xt = sb("xs_t", [P, 2, 2, P])
        hid = sb("hidden", [P, 2, HC, P])
        ys = sb("ys", [P, 2, D])
        above = sb("above", [P, S])

        x_in = [new_sem("x_in0"), new_sem("x_in1")]
        w1_in = [new_sem("w1_in0"), new_sem("w1_in1")]
        w2_in = [new_sem("w2_in0"), new_sem("w2_in1")]
        y_out = [new_sem("y_out0"), new_sem("y_out1")]
        ones_rows, t_full, t_ready = new_sem("ones_rows5"), new_sem("xs_t_full"), new_sem("xs_t_ready")
        up_done, act_done, down_done, y_ready = new_sem("up_done"), new_sem("gelu_done"), new_sem("down_done"), new_sem("y_ready")
        ranked, pool_held, y_free = new_sem("ranked"), new_sem("pool5_held"), new_sem("y_free")
        loaded = new_sem("sp5_held")

        def tbank(u):
            return PSB[:, 4 + u, :]

        def ybank(u):
            return PSB[:, 6 + u, 0:D]

        def hbank(u):
            return PSB[:, 2 * u:2 * u + 2, 0:HROW]

        def xrows(s):
            return io["sorted_x"][bass.ds(s * P, P), :]

        with nc.Block() as block:
            @block.sync
            def _(sp):
                def load_x(s, u):
                    sp.dma_start(xs[:, u, :], xrows(s)).then_inc(x_in[u], 16)

                def load_w1(e, u):
                    sp.dma_start(w1a[:, u, :], io["W1"][bass.ds(e, 1), 0:P, :].rearrange("o p n -> (o p) n")).then_inc(w1_in[u], 16)
                    sp.dma_start(w1b[0:D1, u, :], io["W1"][bass.ds(e, 1), P:D, :].rearrange("o p n -> (o p) n")).then_inc(w1_in[u], 16)
                    sp.dma_start(w1b[D1:D1 + 1, u, :], io["b1"][bass.ds(e, 1), :]).then_inc(w1_in[u], 16)

                def load_w2(e, u):
                    sp.dma_start(w2[:, u, :, :], io["W2"][bass.ds(e, 1), :, :].rearrange("o (m p) n -> (o p) m n", p=P)).then_inc(w2_in[u], 16)
                    sp.dma_start(b2[:, u, :], io["b2"][bass.ds(e, 1), :].broadcast_to([P, D])).then_inc(w2_in[u], 16)

                def expert_of(s):
                    return sp.value_load(mem["tile_expert"][0:1, bass.ds(s, 1)], min_val=0, max_val=E - 1)

                for s in range(2):
                    e = expert_of(s)
                    load_x(s, s)
                    load_w1(e, s)
                    load_w2(e, s)
                with sp.Fori(0, SLOTS // 2 - 1) as i:
                    for u in range(2):
                        s = 2 * i + 2 + u
                        e = expert_of(s)
                        hold(sp, t_full, 2 * i + 1 + u, loaded)
                        load_x(s, u)
                        hold(sp, up_done, 2 * i + 1 + u, loaded)
                        load_w1(e, u)
                        hold(sp, y_ready, 2 * i + 1 + u, loaded)
                        load_w2(e, u)

            @block.tensor
            def _(pe):
                def turn(s, u, i):
                    pe.wait_ge(x_in[u], (i + 1) * 16)
                    pe.transpose(tbank(u)[:, 0:P], xs[:, u, 0:P], ident[:, :])
                    pe.transpose(tbank(u)[0:D1, P:2 * P], xs[:, u, P:D], ident[:, :]).then_inc(t_full, 1)

                def up(s, u, i):
                    pe.wait_ge(w1_in[u], (i + 1) * 48)
                    pe.wait_ge(t_ready, 2 * s + 2)
                    for m in range(HC):
                        dst = PSB[:, 2 * u + m // (HC // 2), m % (HC // 2) * P:(m % (HC // 2) + 1) * P]
                        pe.matmul(dst, w1a[:, u, m * P:(m + 1) * P], xt[:, u, 0, :], start=True, stop=False)
                        mm = pe.matmul(dst, w1b[:, u, m * P:(m + 1) * P], xt[0:D1 + 1, u, 1, :], start=False, stop=True)
                    mm.then_inc(up_done, 1)

                def down(s, u, i):
                    pe.wait_ge(w2_in[u], (i + 1) * 32)
                    pe.wait_ge(act_done, s + 1)
                    for m in range(HC):
                        mm = pe.matmul(ybank(u), hid[:, u, m, :], w2[:, u, m, :], start=m == 0, stop=m == HC - 1)
                    mm.then_inc(down_done, 1)

                pe.wait_ge(ones_rows, 2)
                turn(0, 0, 0)
                up(0, 0, 0)
                turn(1, 1, 0)
                with pe.Fori(0, SLOTS // 2 - 1) as i:
                    s = 2 * i
                    up(s + 1, 1, i)
                    turn(s + 2, 0, i + 1)
                    down(s, 0, i)
                    up(s + 2, 0, i + 1)
                    turn(s + 3, 1, i + 1)
                    down(s + 1, 1, i)
                last = SLOTS // 2 - 1
                up(SLOTS - 1, 1, last)
                down(SLOTS - 2, 0, last)
                down(SLOTS - 1, 1, last)

            @block.scalar
            def _(act):
                with act.Fori(0, SLOTS // 2) as i:
                    for u in range(2):
                        act.wait_ge(up_done, 2 * i + u + 1)
                        act.activation(hid[:, u, :, :].rearrange("p (a m) t -> p a (m t)", a=2), hbank(u), ACT.Gelu_apprx_tanh).then_inc(act_done, 1)

            @block.vector
            def _(dve):
                for u in range(2):
                    dve.memset(xt[D1:D1 + 1, u, 1, :], 1.0).then_inc(ones_rows, 1)

                def tile(i, u):
                    s = 2 * i + u
                    dve.wait_ge(t_full, s + 1)
                    dve.tensor_copy(xt[:, u, 0, :], tbank(u)[:, 0:P]).then_inc(t_ready, 1)
                    dve.tensor_copy(xt[0:D1, u, 1, :], tbank(u)[0:D1, P:2 * P]).then_inc(t_ready, 1)

                def finish(s, u, i):
                    dve.wait_ge(y_free, s + 1)
                    dve.wait_ge(down_done, s + 1)
                    dve.tensor_tensor(ys[:, u, :], ybank(u), b2[:, u, :], ALU.add).then_inc(y_ready, 1)

                tile(0, 0)
                with dve.Fori(0, SLOTS // 2 - 1) as i:
                    tile(i, 1)
                    finish(2 * i, 0, i)
                    tile(i + 1, 0)
                    finish(2 * i + 1, 1, i)
                last = SLOTS // 2 - 1
                tile(last, 1)
                finish(SLOTS - 2, 0, last)
                finish(SLOTS - 1, 1, last)
                k = Count(ranked)
                for t in range(NT):
                    if t:
                        dve.wait_ge(ranked, t)
                    k.on(dve.tensor_scalar(above[:, :], SB[:, t // TB, :], score[:, t:t + 1], None, ALU.is_gt, ALU.add,
                                           accum_out=rank[:, t:t + 1]))

            @block.gpsimd
            def _(pool):
                pool.sem_inc(y_free, 2)
                with pool.Fori(0, SLOTS // 2) as i:
                    for u in range(2):
                        hold(pool, y_ready, 2 * i + u + 1, pool_held)
                        pool.dma_start(io["sorted_y"][bass.ds((2 * i + u) * P, P), :], ys[:, u, :]).then_inc(y_out[u], 16)
                        pool.wait_ge(y_out[u], i * 16 + 16)
                        pool.sem_inc(y_free, 1)
                for u in range(2):
                    pool.wait_ge(y_out[u], SLOTS // 2 * 16)


LEN, WARM = 8, 24
SPAN = 2 * LEN
WIN = SPAN + 2 * WARM
ROUNDS = WARM + LEN


def finish(nc, io, mem, new_sem, out):
    H, PSB, ident = mem["H"], mem["PSB"], mem["ident"]
    Y, FFN = mem["VALL"], mem["AO"]
    top_p, rank, dest = mem["top_p"], mem["rank"], mem["dest"]
    with ExitStack() as ctx:
        def sb(name, shape, dt=fp32):
            return ctx.enter_context(nc.sbuf_tensor(name, shape, dt))

        wv, wo2, fbo = sb("wv_row", [P, D]), sb("feature_rows", [P, 2, D]), sb("feature_bias", [P, D])
        bv, bk = sb("v_bias", [P, 1]), sb("bk_scale_sb", [P, 1])
        prod = sb("v_products", [P, 2, D])
        v, mask = sb("v", [P, NT]), sb("mask", [P, NT])
        vT = sb("vT", [NT, P])
        edge = sb("edge", [B, 2, PAD])
        win = sb("windows", [P, B, WIN])
        drive = sb("drive", [P, ROUNDS, 2, B, 2, 2])
        state = sb("state", [P, ROUNDS + 1, 2, B, 2, 2])
        sq, den, inv = sb("squares", [P, 2, B, 2, 2]), sb("norms", [P, 2, B, 2]), sb("norm_rcp", [P, 2, B, 2])
        turn = sb("turned_state", [P, 2, B, 2, 2])
        sign = sb("signs", [P, B, 2, LEN])
        cr, ci, c2, cd = (sb(n, [P, B, 2, LEN]) for n in ("c_real", "c_imag", "c_square", "c_norm"))
        g = sb("g", [P, 2, B, 2, LEN])
        gT = sb("gT", [NT, 2, P])
        gp = sb("g_tokens", [P, 2, NT])
        row = sb("out_rows", [P, NT, D])

        c_in, gathered = new_sem("c6_in"), new_sem("y_gathered")
        dve_done, tv_full, vT_ready = new_sem("dve6_done"), new_sem("vT_full"), new_sem("vT_ready")
        edge_ready, pot_out, win_in = new_sem("edge_ready"), new_sem("potential_out"), new_sem("windows_in")
        g_ready, g_out, gT_in, gp_full, row_ready, stored = (new_sem(n) for n in (
            "g_ready", "g_out", "gT_in", "gp_full", "row_ready", "stored"))
        v_ready = new_sem("v_ready")
        tb = PSB[:, 0, :]

        with nc.Block() as block:
            @block.sync
            def _(sp):
                def all_rows(a, n):
                    return a.rearrange("(o n) -> o n", o=1).broadcast_to([P, n])
                sp.dma_start(wv[:, :], all_rows(io["fWv"], D)).then_inc(c_in, 16)
                sp.dma_start(wo2[:, :, :].rearrange("p a n -> p (a n)"), all_rows(io["fWo"].rearrange("a n -> (a n)"), 2 * D)).then_inc(c_in, 16)
                sp.dma_start(fbo[:, :], all_rows(io["fbo"], D)).then_inc(c_in, 16)
                sp.dma_start(bv[:, :], all_rows(io["fbv"], 1)).then_inc(c_in, 16)
                sp.dma_start(bk[:, :], all_rows(io["bk_scale"], 1)).then_inc(c_in, 16)
                sp.wait_ge(edge_ready, 3)
                sp.dma_start(io["potential"][:, 0:PAD], edge[:, 0, :]).then_inc(pot_out, 16)
                sp.dma_start(io["potential"][:, PAD + S:PAD + S + PAD], edge[:, 1, :]).then_inc(pot_out, 16)
                sp.wait_ge(vT_ready, 1)
                for b in range(B):
                    sp.dma_start(io["potential"][b, PAD:PAD + S].rearrange("(t p) -> t p", p=P), vT[b * TB:(b + 1) * TB, :]).then_inc(pot_out, 16)
                sp.wait_ge(pot_out, 64)
                for b in range(B):
                    src = bass.AP(tensor=io["potential"].tensor, offset=b * (2 * PAD + S) + PAD - WARM, ap=[[SPAN, P], [1, WIN]])
                    sp.dma_start(win[:, b, :], src).then_inc(win_in, 16)
                sp.wait_ge(g_ready, 2)
                for a in range(2):
                    sp.dma_start(io["green"][a].rearrange("b (p n) -> p b n", p=P), g[:, a, :, :, :].rearrange("p b m r -> p b (m r)")).then_inc(g_out, 16)
                sp.wait_ge(g_out, 32)
                for a in range(2):
                    sp.dma_start(gT[:, a, :], io["green"][a].rearrange("b (t p) -> (b t) p", p=P)).then_inc(gT_in, 16)
                for q in range(NQ):
                    sp.wait_ge(row_ready, QUAD * (q + 1))
                    b, t = divmod(QUAD * q, TB)
                    sp.dma_start(out[b, t * P:(t + QUAD) * P, :].rearrange("(t p) d -> p t d", p=P), row[:, QUAD * q:QUAD * q + QUAD, :]).then_inc(stored, 16)
                sp.wait_ge(stored, 16 * NQ)

            @block.gpsimd
            def _(pool):
                for q in range(NQ):
                    for t in range(QUAD * q, QUAD * q + QUAD):
                        pool.indirect_dma_start(Y[:, t, :], None, io["sorted_y"][:, :],
                                                bass.IndirectOffsetOnAxis(dest[:, t:t + 1], 0)).then_inc(gathered, 16)

            @block.tensor
            def _(pe):
                pe.wait_ge(v_ready, 1)
                pe.transpose(tb[0:NT, 0:P], v[:, :], ident[:, :]).then_inc(tv_full, 1)
                pe.wait_ge(vT_ready, 1)
                pe.wait_ge(gT_in, 32)
                for a in range(2):
                    mm = pe.transpose(tb[:, a * NT:(a + 1) * NT], gT[:, a, :], ident[0:NT, 0:NT])
                mm.then_inc(gp_full, 1)

            @block.vector
            def _(dve):
                k = Count(dve_done)
                dve.memset(edge[:, :, :], 0.0).then_inc(edge_ready, 1)
                dve.wait_ge(edge_ready, 1)
                dve.memset(edge[:, 0, PAD - 1:PAD], 1e18).then_inc(edge_ready, 1)
                dve.memset(edge[:, 1, 0:1], 1e18).then_inc(edge_ready, 1)
                k.on(dve.memset(drive[:, :, :, :, :, 1], 1.0))
                k.on(dve.memset(state[:, 0, :, :, :, 0], 0.0))
                k.on(dve.memset(state[:, 0, :, :, :, 1], 1.0))
                k.on(dve.memset(sign[:, :, :, 0:LEN:2], 1.0))
                k.on(dve.memset(sign[:, :, :, 1:LEN:2], -1.0))
                dve.wait_ge(c_in, 80)
                dve.wait_ge(gathered, 16 * NT)
                for t in range(NT):
                    if t >= 2:
                        dve.wait_ge(dve_done, k.n - 2)
                    k.on(dve.tensor_scalar(FFN[:, t, :], Y[:, t, :], top_p[:, t:t + 1], None, ALU.mult))
                    dve.wait_ge(dve_done, k.n)
                    k.on(dve.tensor_tensor_reduce(prod[:, t % 2, :], FFN[:, t, :], wv[:, :], 1.0, 0.0, ALU.mult, ALU.add, v[:, t:t + 1]))
                dve.wait_ge(dve_done, k.n)
                k.chain(dve, dve.tensor_scalar(v[:, :], v[:, :], bv[:, 0:1], -V_MAX, ALU.add, ALU.max))
                dve.tensor_scalar(v[:, :], v[:, :], V_MAX, None, ALU.min).then_inc(v_ready, 1)
                dve.wait_ge(tv_full, 1)
                dve.tensor_copy(vT[:, :], tb[0:NT, 0:P]).then_inc(vT_ready, 1)
                k.on(dve.tensor_scalar(fbo[:, :], fbo[:, :], bk[:, 0:1], None, ALU.mult))
                k.on(dve.tensor_scalar(wo2[:, :, :], wo2[:, :, :], bk[:, 0:1], None, ALU.mult))
                k.on(dve.tensor_scalar(mask[:, :], rank[:, :], float(KEEP), None, ALU.is_lt))
                k.chain(dve, dve.tensor_tensor(row[:, :, :], H[:, :, :], FFN[:, :, :], ALU.add))
                k.chain(dve, dve.tensor_tensor(row[:, :, :], row[:, :, :], fbo[:, :].unsqueeze(1).broadcast_to([P, NT, D]), ALU.add))
                dve.wait_ge(win_in, 32)
                for m in range(2):
                    for par in range(2):
                        f = win[:, :, LEN * m + par:LEN * m + ROUNDS:2]
                        k.on(dve.tensor_scalar(drive[:, par::2, 0, :, m, 0], f.rearrange("p b k -> p k b"), 1.0 - 2 * par, None, ALU.mult))
                        top = LEN * m + WARM + ROUNDS - 1 - par
                        for kk in range(ROUNDS // 2):
                            last = k.on(dve.tensor_scalar(drive[:, par + 2 * kk, 1, :, m, 0], win[:, :, top - 2 * kk], 1.0 - 2 * par, None, ALU.mult))
                dve.wait_ge(dve_done, last)
                for s in range(ROUNDS):
                    now = state[:, s, :, :, :, :]
                    k.chain(dve, dve.tensor_tensor(sq[:, :, :, :, :], now, now, ALU.mult))
                    k.chain(dve, dve.tensor_tensor(den[:, :, :, :], sq[:, :, :, :, 0], sq[:, :, :, :, 1], ALU.add))
                    k.chain(dve, dve.reciprocal(inv[:, :, :, :], den[:, :, :, :]))
                    k.chain(dve, dve.tensor_tensor(turn[:, :, :, :, :], now, inv[:, :, :, :].unsqueeze(4).broadcast_to([P, 2, B, 2, 2]), ALU.mult))
                    k.chain(dve, dve.tensor_tensor(state[:, s + 1, :, :, :, :], turn[:, :, :, :, :], drive[:, s, :, :, :, :], ALU.add))
                for r in range(LEN):
                    f, w = state[:, WARM + 1 + r, 0, :, :, :], state[:, ROUNDS - r, 1, :, :, :]
                    k.on(dve.tensor_tensor(cr[:, :, :, r], f[:, :, :, 0], w[:, :, :, 0], ALU.subtract))
                    k.on(dve.scalar_tensor_tensor(out=ci[:, :, :, r], in0=f[:, :, :, 1], scalar=-1.0, in1=w[:, :, :, 1], op0=ALU.add, op1=ALU.add))
                dve.wait_ge(dve_done, k.n)
                k.chain(dve, dve.tensor_tensor(cr[:, :, :, :], cr[:, :, :, :], sign[:, :, :, :], ALU.mult))
                k.chain(dve, dve.tensor_tensor(cr[:, :, :, :], cr[:, :, :, :], win[:, :, WARM:WARM + SPAN].rearrange("p b (m r) -> p b m r", m=2), ALU.subtract))
                k.chain(dve, dve.tensor_tensor(c2[:, :, :, :], cr[:, :, :, :], cr[:, :, :, :], ALU.mult))
                k.chain(dve, dve.tensor_tensor(cd[:, :, :, :], ci[:, :, :, :], ci[:, :, :, :], ALU.mult))
                k.chain(dve, dve.tensor_tensor(cd[:, :, :, :], cd[:, :, :, :], c2[:, :, :, :], ALU.add))
                k.chain(dve, dve.reciprocal(cd[:, :, :, :], cd[:, :, :, :]))
                dve.tensor_tensor(g[:, 0, :, :, :], cr[:, :, :, :], cd[:, :, :, :], ALU.mult).then_inc(g_ready, 1)
                dve.tensor_tensor(g[:, 1, :, :, :], ci[:, :, :, :], cd[:, :, :, :], ALU.mult).then_inc(g_ready, 1)
                dve.wait_ge(gp_full, 1)
                for a in range(2):
                    last = k.on(dve.tensor_tensor(gp[:, a, :], tb[:, a * NT:(a + 1) * NT], mask[:, :], ALU.mult))
                dve.wait_ge(dve_done, last)
                k.chain(dve, dve.tensor_scalar(gp[:, :, :], gp[:, :, :], -FEAT_CLAMP, FEAT_CLAMP, ALU.max, ALU.min))
                for t in range(NT):
                    k.chain(dve, dve.scalar_tensor_tensor(out=row[:, t, :], in0=wo2[:, 0, :], scalar=gp[:, 0, t:t + 1], in1=row[:, t, :], op0=ALU.mult, op1=ALU.add))
                    dve.scalar_tensor_tensor(out=row[:, t, :], in0=wo2[:, 1, :], scalar=gp[:, 1, t:t + 1], in1=row[:, t, :], op0=ALU.mult, op1=ALU.add).then_inc(row_ready, 1)


def lm_tower(nc, io, out):
    with ExitStack() as c:
        def sb(name, shape, dt=fp32):
            return c.enter_context(nc.sbuf_tensor(name, shape, dt))

        def new_sem(name):
            return c.enter_context(nc.semaphore(name))

        for name, shape, dt in (("sorted_x", [SLOTS * P, D], fp32), ("sorted_y", [SLOTS * P, D], fp32),
                                ("score_rows", [B, S], fp32), ("potential", [B, PAD + S + PAD], fp32),
                                ("green", [2, B, S], fp32)):
            io[name] = nc.dram_tensor(name, shape, dt, kind="Internal").ap()
        mem = {
            "H": sb("H", [P, NT, D]),
            "VALL": sb("VALL", [P, NT, D]),
            "AO": sb("AO", [P, NT, D]),
            "ident": sb("ident", [P, P]), "ident16": sb("ident16", [P, P], fp16), "identb": sb("identb", [P, P], bf16),
            "masks": sb("masks", [P, 2, P], bf16), "minus_half": sb("minus_half", [P, NT]),
            "before": sb("before", [P, P]), "ones": sb("ones", [P, P]),
            "PSB": c.enter_context(nc.psum_tensor("PSB", [P, 8, 512], fp32)),
        }
        with ExitStack() as a:
            mem["XT0"] = a.enter_context(nc.sbuf_tensor("XT0", [P, N], fp32))
            mem["XT1"] = a.enter_context(nc.sbuf_tensor("XT1", [D1 + 1, N], fp32))
            embed_and_project_values(nc, io, mem, new_sem)
            attention(nc, io, mem, new_sem)
        mem["LG"] = sb("LG", [P, NT, GATES])
        for name in ("top_p", "score", "rank"):
            mem[name] = sb(name, [P, NT])
        mem["dest"] = sb("dest", [P, NT], i32)
        mem["tile_expert"] = sb("tile_expert", [1, SLOTS], i32)
        mem["score_all"] = sb("score_all", [P, B, S])
        mix_and_norm(nc, io, mem, new_sem)
        route(nc, io, mem, new_sem)
        experts(nc, io, mem, new_sem)
        finish(nc, io, mem, new_sem, out)


PAD = 32


_INS = {"x": "x", "seg": "mask_BS_i2_0", "tok": "L0_tok_token_table", "segm": "L0_tok_segm_table",
        "Wq": "L0_attn_Wq", "bq": "L0_attn_bq", "Wk": "L0_attn_Wk", "bk": "L0_attn_bk",
        "Wv": "L0_attn_Wv", "bv": "L0_attn_bv", "Wo": "L0_attn_Wo", "bo": "L0_attn_bo",
        "Wg": "L0_ffn_Wg", "bg": "L0_ffn_bg", "W1": "L0_ffn_W1", "b1": "L0_ffn_b1",
        "W2": "L0_ffn_W2", "b2": "L0_ffn_b2", "fWv": "L0_ffn_Wv", "fbv": "L0_ffn_bv",
        "Wm": "L0_ffn_Wm", "bm": "L0_ffn_bm", "fWo": "L0_ffn_Wo", "fbo": "L0_ffn_bo",
        "bk_scale": "L0_ffn_bk_scale"}


def shape_constants():
    import numpy as np
    f = np.float32
    pos = np.arange(S, dtype=f)[:, None]
    ids = np.arange(D, dtype=f)
    angle = pos / np.power(10000.0, (np.floor(ids / f(2)) * f(2) / f(D)).astype(np.float64)).astype(f)[None, :]
    table = np.where(np.arange(D) % 2 == 0, np.sin(angle.astype(np.float64)), np.cos(angle.astype(np.float64))).astype(f)
    half = np.arange(D // 2, dtype=f) * f(2) / f(D)
    turn = pos * (f(1) / np.power(10000.0, half.astype(np.float64)).astype(f))[None, :]
    cos = np.repeat(np.cos(turn.astype(np.float64)), 2, 1).T.astype(f)
    sin = np.repeat(np.sin(turn.astype(np.float64)), 2, 1).T.astype(f)
    sin[0::2] *= -1
    rope = np.stack([cos, sin], 1).reshape(G, 1, GD, 2, NCH, CH)
    rope = np.broadcast_to(rope, (G, 2, GD, 2, NCH, CH)).transpose(0, 4, 1, 2, 3, 5).reshape(G * NCH, P, 2, CH)
    return {"pos": np.ascontiguousarray(table.reshape(TB, P, D).transpose(1, 0, 2)), "rope": np.ascontiguousarray(rope)}


def kernel(**inputs):
    import numpy as _np
    import concourse.bacc as _bacc
    from concourse import mybir as _mybir
    from concourse.bass_utils import run_bass_kernel_spmd as _run

    nc = _bacc.Bacc("TRN2", target_bir_lowering=False, num_devices=1)
    arrays, io = {}, {}
    given = {name: _np.ascontiguousarray(inputs[source]) for name, source in _INS.items()}
    for name, a in {**given, **shape_constants()}.items():
        a = a.reshape(a.shape or (1,))
        arrays[f"in_{name}"] = a
        io[name] = nc.dram_tensor(f"in_{name}", a.shape, _mybir.dt.from_np(a.dtype), kind="ExternalInput").ap()
    out = nc.dram_tensor("out_h", [B, S, D], _mybir.dt.float32, kind="ExternalOutput").ap()
    lm_tower(nc, io, out)
    r = _run(nc, [arrays], core_ids=[0])
    return r.results[0]["out_h"]
```

```python
import concourse.bass as bass
from concourse import mybir
from contextlib import ExitStack

fp32 = mybir.dt.float32
fp16 = mybir.dt.float16
bf16 = mybir.dt.bfloat16
i32 = mybir.dt.int32
ALU = mybir.AluOpType
ACT = mybir.ActivationFunctionType
AX = mybir.AxisListType

P = 128
B, S = 2, 2048
N = B * S
D = 192
D1 = D - P
NT = N // P
TB = S // P
QUAD = 4
NQ = NT // QUAD
HEADS, HD = 12, 16
GH = 4
G = HEADS // GH
GD = GH * HD
CH = 512
NCH = S // CH
CT = CH // P
KROWS = 3 * HD
VOCAB, SEGS = 8000, 3
E, HID = 8, 768
HC = HID // P
EPS = 1e-5
KEEP = int(512 * (1.0 - 0.6))
V_MAX, FEAT_CLAMP = 3.0, 10.0
NEG = -1e30
SLOTS = NT + E


START = 1


class Count:

    def __init__(self, sem, base=0):
        self.sem, self.base, self.n = sem, base, 0

    def on(self, instruction, by=1):
        instruction.then_inc(self.sem, by)
        self.n += by
        return self.base + self.n

    def chain(self, engine, instruction):
        engine.wait_ge(self.sem, self.on(instruction))


def hold(engine, sem, value, held):
    engine.wait_ge(sem, value)
    engine.sem_inc(held, 1)


def embed_and_project_values(nc, io, mem, new_sem):
    H, XT0, XT1, VALL, POS, PSB = mem["H"], mem["XT0"], mem["XT1"], mem["VALL"], mem["AO"], mem["PSB"]
    ident = mem["ident"]
    with ExitStack() as c:
        def sb(name, shape, dt=fp32):
            return c.enter_context(nc.sbuf_tensor(name, shape, dt))

        raw = sb("raw_ids", [NT, 2, P], i32)
        rawf = sb("raw_ids_f", [NT, 2, P])
        wrap = sb("wrap", [NT, P])
        tok_f = sb("tok_f", [P, NT])
        tok_i = sb("tok_i", [P, NT], i32)
        lab_f = sb("lab_f", [P, NT])
        one_hot = sb("label_one_hot", [P, SEGS, NT])
        seg_rows = sb("seg_rows", [P, SEGS, D])
        wv0 = sb("wv0", [P, D])
        wv1 = sb("wv1", [D1 + 1, D])
        stats = sb("ln1_stats", [P, QUAD, 6])
        mv = sb("ln1_mean_var", [P, QUAD, 2])
        var_eps = sb("ln1_var_eps", [P, QUAD])
        rstd = sb("ln1_rstd", [P, QUAD])
        minus_half = mem["minus_half"]
        xn = sb("ln1_out", [P, QUAD, D])
        xq0 = sb("xq0", [P, QUAD * P])
        xq1 = sb("xq1", [D1 + 1, QUAD * P])
        zero = sb("zero_rows", [P, 2 * D])

        ids_in, tab_in, zeroed = new_sem("ids_in"), new_sem("tab_in"), new_sem("zeroed")
        zero_ready, ones_rows, pool_done = new_sem("zero_ready"), new_sem("ones_rows_ready"), new_sem("pool1_done")
        held, act_held = new_sem("dve1_held"), new_sem("act1_held")
        ids_t, ids_ready = new_sem("ids_transposed"), new_sem("ids_ready")
        gathered, rows_ready = new_sem("gathered"), new_sem("rows_ready")
        dve_done = new_sem("dve1_done")
        var_ready, rstd_ready = new_sem("var1_ready"), new_sem("rstd1_ready")
        xn_ready, xt_full, xt_free = new_sem("xn1_ready"), new_sem("xt1_full"), new_sem("xt1_free")
        xq_ready, xt_kept = new_sem("xq_ready"), new_sem("xt1_kept")
        v_full, v_kept = new_sem("v_full"), new_sem("v_kept")
        t0 = PSB[:, 0, :]
        t1 = PSB[:, 1, :]
        vp = PSB[:, 2:4, :].rearrange("p a (k n) -> p (a k) n", k=2)

        with nc.Block() as block:
            @block.sync
            def _(sp):
                sp.dma_start(raw[:, 0, :], io["x"].rearrange("b (t p) -> (b t) p", p=P)).then_inc(ids_in, 16)
                sp.dma_start(raw[:, 1, :], io["seg"].rearrange("b (t p) -> (b t) p", p=P)).then_inc(ids_in, 16)
                sp.dma_start(seg_rows[:, :, :].rearrange("p s d -> p (s d)"),
                             io["segm"].rearrange("s d -> (s d)").rearrange("(o n) -> o n", o=1)
                             .broadcast_to([P, SEGS * D])).then_inc(tab_in, 16)
                sp.dma_start(POS[:, 0:TB, :], io["pos"]).then_inc(tab_in, 16)
                sp.dma_start(wv0[:, :], io["Wv"][0:P, :]).then_inc(tab_in, 16)
                sp.dma_start(wv1[0:D1, :], io["Wv"][P:D, :]).then_inc(tab_in, 16)
                sp.dma_start(wv1[D1:D1 + 1, :], io["bv"].rearrange("(o n) -> o n", o=1)).then_inc(tab_in, 16)
                sp.wait_ge(zero_ready, 1)
                slots = io["sorted_x"].rearrange("(a p two) d -> a p (two d)", p=P, two=2)
                for a in range(SLOTS // 2):
                    sp.dma_start(slots[a], zero[:, :]).then_inc(zeroed, 16)
                sp.wait_ge(zeroed, 16 * (SLOTS // 2))

            @block.gpsimd
            def _(pool):
                k = Count(pool_done)
                pool.memset(zero[:, :], 0.0).then_inc(zero_ready, 1)
                k.chain(pool, pool.memset(ident[:, :], 0.0))
                k.chain(pool, pool.affine_select(out=ident[:, :], in_=ident[:, :], compare_op=ALU.not_equal,
                                                 fill=1.0, base=0, pattern=[[-1, P]], channel_multiplier=1))
                k.chain(pool, pool.tensor_copy(mem["ident16"][:, :], ident[:, :]))
                k.chain(pool, pool.tensor_copy(mem["identb"][:, :], ident[:, :]))
                k.chain(pool, pool.memset(mem["masks"][:, :, :], 0.0))
                k.chain(pool, pool.affine_select(out=mem["masks"][:, 0, :], in_=mem["masks"][:, 0, :],
                                                 compare_op=ALU.is_ge, fill=NEG, base=0,
                                                 pattern=[[-1, P]], channel_multiplier=1))
                k.chain(pool, pool.affine_select(out=mem["masks"][:, 1, :], in_=mem["masks"][:, 1, :],
                                                 compare_op=ALU.is_ge, fill=NEG, base=0,
                                                 pattern=[[1, P]], channel_multiplier=-1))
                k.chain(pool, pool.memset(minus_half[:, :], -0.5))
                k.chain(pool, pool.memset(mem["before"][:, :], 1.0))
                k.chain(pool, pool.affine_select(out=mem["before"][:, :], in_=mem["before"][:, :],
                                                 compare_op=ALU.is_gt, fill=0.0, base=0,
                                                 pattern=[[1, P]], channel_multiplier=-1))
                k.chain(pool, pool.memset(mem["ones"][:, :], 1.0))

                def reciprocal_root(q):
                    pool.wait_ge(var_ready, q + 1)
                    pool.tensor_tensor(rstd[:, :], var_eps[:, :], minus_half[:, 0:QUAD], ALU.pow).then_inc(rstd_ready, 1)

                pool.wait_ge(ids_ready, 1)
                for q in range(NQ):
                    for t in range(QUAD * q, QUAD * q + QUAD):
                        pool.indirect_dma_start(H[:, t, :], None, io["tok"][:, :],
                                                bass.IndirectOffsetOnAxis(tok_i[:, t:t + 1], 0)).then_inc(gathered, 16)
                    pool.wait_ge(gathered, 16 * QUAD * (q + 1))
                    pool.sem_inc(rows_ready, 1)
                    if q:
                        reciprocal_root(q - 1)
                reciprocal_root(NQ - 1)

            @block.vector
            def _(dve):
                k = Count(dve_done)
                dve.memset(XT1[D1:D1 + 1, :], 1.0).then_inc(ones_rows, 1)
                dve.memset(xq1[D1:D1 + 1, :], 1.0).then_inc(ones_rows, 1)
                dve.wait_ge(ids_in, 32)
                k.chain(dve, dve.tensor_copy(rawf[:, :, :], raw[:, :, :]))
                for n, rows in ((0, VOCAB), (1, SEGS)):
                    k.chain(dve, dve.tensor_scalar(wrap[:, :], rawf[:, n, :], 0.0, float(rows), ALU.is_lt, ALU.mult))
                    k.chain(dve, dve.tensor_tensor(rawf[:, n, :], rawf[:, n, :], wrap[:, :], ALU.add))
                    k.chain(dve, dve.tensor_scalar(rawf[:, n, :], rawf[:, n, :], 0.0, float(rows - 1), ALU.max, ALU.min))
                dve.wait_ge(ids_t, 1)
                k.chain(dve, dve.tensor_copy(tok_f[:, :], t0[:, 0:NT]))
                dve.tensor_copy(tok_i[:, :], tok_f[:, :]).then_inc(ids_ready, 1)
                k.chain(dve, dve.tensor_copy(lab_f[:, :], t0[:, NT:2 * NT]))
                for s in range(SEGS):
                    k.chain(dve, dve.tensor_scalar(one_hot[:, s, :], lab_f[:, :], float(s), None, ALU.is_equal))
                dve.wait_ge(tab_in, 80)
                dve.sem_inc(xq_ready, START)
                before = k.n
                with dve.Fori(0, B) as b, dve.Fori(0, NQ // B) as r:
                    q = b * (NQ // B) + r
                    k = Count(dve_done, before + q * DVE1)
                    dve.wait_ge(rows_ready, q + 1)
                    h = H[:, bass.ds(q * QUAD, QUAD), :]
                    k.chain(dve, dve.tensor_tensor(h, h, POS[:, bass.ds(r * QUAD, QUAD), :], ALU.add))
                    for s in range(SEGS):
                        for t in range(QUAD):
                            ht = H[:, bass.ds(q * QUAD + t, 1), :].rearrange("p o d -> p (o d)")
                            last = k.on(dve.scalar_tensor_tensor(
                                out=ht, in0=seg_rows[:, s, :], scalar=one_hot[:, s, bass.ds(q * QUAD + t, 1)],
                                in1=ht, op0=ALU.mult, op1=ALU.add))
                        hold(dve, dve_done, last, held)
                    for t in range(QUAD):
                        last = k.on(dve.bn_stats(stats[:, t, :], H[:, bass.ds(q * QUAD + t, 1), :].rearrange("p o d -> p (o d)")))
                    hold(dve, dve_done, last, held)
                    for t in range(QUAD):
                        last = k.on(dve.bn_aggr(mv[:, t, :], stats[:, t, :]))
                    dve.wait_ge(dve_done, last)
                    dve.tensor_scalar(var_eps[:, :], mv[:, :, 1], EPS, None, ALU.add).then_inc(var_ready, 1)
                    dve.wait_ge(rstd_ready, q + 1)
                    for t in range(QUAD):
                        k.on(dve.tensor_scalar(xn[:, t, :], H[:, bass.ds(q * QUAD + t, 1), :].rearrange("p o d -> p (o d)"),
                                               mv[:, t, 0:1], rstd[:, t:t + 1], ALU.subtract, ALU.mult))
                    assert k.n == DVE1, k.n
                    dve.wait_ge(xt_full, q + 1)
                    dve.wait_ge(xt_kept, q + START)
                    dve.wait_ge(v_full, q + START)
                    dve.tensor_scalar(xq0[:, :], t0, 1.0, None, ALU.mult).then_inc(xq_ready, 1)
                    dve.tensor_scalar(xq1[0:D1, :], t1[0:D1, :], 1.0, None, ALU.mult).then_inc(xq_ready, 1)

            @block.tensor
            def _(pe):
                pe.wait_ge(ones_rows, 2)
                pe.wait_ge(pool_done, POOL1)
                pe.wait_ge(dve_done, 7)
                pe.transpose(t0[:, 0:NT], rawf[:, 0, :], ident[0:NT, 0:NT])
                pe.transpose(t0[:, NT:2 * NT], rawf[:, 1, :], ident[0:NT, 0:NT]).then_inc(ids_t, 1)
                pe.wait_ge(tab_in, 80)
                pe.sem_inc(v_full, START)
                with pe.Fori(0, NQ) as q:
                    pe.wait_ge(xq_ready, 2 * q + START)
                    pe.wait_ge(dve_done, DVE1_HEAD + (q + 1) * DVE1)
                    for t in range(QUAD):
                        pe.transpose(t0[:, t * P:(t + 1) * P], xn[:, t, 0:P], ident[:, :])
                    for t in range(QUAD):
                        last = pe.transpose(t1[0:D1, t * P:(t + 1) * P], xn[:, t, P:D], ident[:, :])
                    last.then_inc(xt_full, 1)
                    pe.wait_ge(v_kept, q + START)
                    pe.wait_ge(xq_ready, 2 * q + 2 + START)
                    for t in range(QUAD):
                        pe.matmul(vp[:, t, 0:D], xq0[:, t * P:(t + 1) * P], wv0[:, :], start=True, stop=False)
                        last = pe.matmul(vp[:, t, 0:D], xq1[:, t * P:(t + 1) * P], wv1[:, :], start=False, stop=True)
                    last.then_inc(v_full, 1)

            @block.scalar
            def _(act):
                act.sem_inc(xt_kept, START)
                act.sem_inc(v_kept, START)
                with act.Fori(0, NQ) as q:
                    hold(act, xq_ready, 2 * q + 2 + START, act_held)
                    act.activation(XT0[:, bass.ds(q * QUAD * P, QUAD * P)], xq0[:, :], ACT.Copy)
                    act.activation(XT1[0:D1, bass.ds(q * QUAD * P, QUAD * P)], xq1[0:D1, :], ACT.Copy).then_inc(xt_kept, 1)
                    hold(act, v_full, q + 1 + START, act_held)
                    act.activation(VALL[:, bass.ds(q * QUAD, QUAD), :], vp[:, :, 0:D], ACT.Copy).then_inc(v_kept, 1)


POOL1 = 10
DVE1 = 1 + SEGS * QUAD + 3 * QUAD
DVE1_HEAD = 12


AHEAD = 3
PEAKS = 2
SHIFT_ROW = 96
PIECES = [CT * GH * (c + 1) for c in range(NCH)]
ALL_PIECES = sum(PIECES)
STEPS = [CT * (c + 1) for c in range(NCH)]
ALL_STEPS = sum(STEPS)


def pieces_before(c):
    return c // NCH * ALL_PIECES + sum(PIECES[:c % NCH])


def steps_before(c):
    return c // NCH * ALL_STEPS + sum(STEPS[:c % NCH])


def last_use(c):
    return steps_before(NCH - 1) + CT * (c % NCH + 1)


def piece(c, n):
    c = c % NCH
    qt, h, kc = n // (GH * (c + 1)), n // (c + 1) % GH, n % (c + 1)
    return qt, h, kc, (qt + 1) * P if kc == c else CH


def first_query(c, j):
    return max(0, j - CT * c) * P


def opening_order():
    order = [(what, c, 0) for c in range(AHEAD) for what in ("project", "rotate")]
    for c in range(PEAKS):
        order += [("max", c, n) for n in range(PIECES[c])] + [(what, c, 0) for what in ("top", "shift", "rows")]
    return order


def round_order(more):
    beside = [[] for _ in range(ALL_STEPS)]

    def pieces(c, first, last):
        total = PIECES[c % NCH]
        for n in range(total):
            beside[first + n * (last - first) // total].append(("max", c, n))
        beside[last].append(("top", c, 0))
        beside[last].append(("shift", c, 0))
        beside[last + 1].insert(0, ("rows", c, 0))

    pieces(2, 0, 10)
    pieces(3, 10, 22)
    if more:
        pieces(4, 30, 34)
        pieces(5, 34, 38)
    for c, k in ((3, 4), (4, 19), (5, 26), (6, 31)):
        if more or c < NCH:
            beside[k].append(("project", c, 0))
            beside[k + 1].insert(0, ("rotate", c, 0))
    order, k = [], 0
    for c in range(NCH):
        for j in range(STEPS[c]):
            items = beside[k]
            quick = [i for i in items if i[0] == "max"]
            slow = [i for i in items if i[0] != "max"]
            if c and j == 1:
                slow = [("norm", c - 1, 0)] + slow
            if c and j == 2:
                slow = [("divide", c - 1, 0)] + slow
            cut = (len(quick) + 1) // 3
            order.append(("scores", c, j))
            order += [("slot", quick[:cut]), ("slot", quick[cut:2 * cut])]
            if k:
                order.append(("values",) + before)
            order += quick[2 * cut:] + slow
            before = (c, j)
            k += 1
    order += [("values",) + before, ("norm", NCH - 1, 0), ("divide", NCH - 1, 0)]
    flat = []
    n = 0
    while n < len(order):
        if order[n][0] == "scores":
            _, c, j = order[n]
            flat += [("scores", c, (j, 0))] + order[n + 1][1] + [("scores", c, (j, 1))] + order[n + 2][1]
            n += 3
        else:
            flat.append(order[n])
            n += 1
    return flat


OPENING = opening_order()
MISC_FIRST = sum(what in ("project", "shift") for what, c, n in OPENING)
MISC = 3 * NCH
DVE2_FIRST = AHEAD + 2 * PEAKS
DVE2 = NCH * 4


def misc_uses(order):
    return {key: n for n, key in enumerate((what, c) for what, c, _ in order if what in ("project", "shift", "norm"))}


def attention(nc, io, mem, new_sem):
    XT0, XT1, VALL, AO, PSB = mem["XT0"], mem["XT1"], mem["VALL"], mem["AO"], mem["PSB"]
    with ExitStack() as ctx:
        def sb(name, shape, dt=fp32):
            return ctx.enter_context(nc.sbuf_tensor(name, shape, dt))

        wq0 = sb("wqk0", [P, 2, GD])
        wq1 = sb("wqk1", [D1 + 1, 2, GD])
        rope = sb("rope", [P, 2, 2, CH])
        xc = sb("x_cos", [P, CH])
        sh = sb("x_turned", [P, CH])
        ss = sb("x_sin", [P, CH])
        rot = sb("rotated", [P, CH])
        split = sb("rotated_split", [P, 2, CH], fp16)
        hi, lo = split[:, 0, :], split[:, 1, :]
        QT = sb("QT", [P, GH, S], fp16)
        KT = sb("KT", [P, GH, S], fp16)
        VG = sb("VG", [P, TB, GH, 32])
        probs = sb("probs", [P, 2, GH, CH])
        tops = sb("piece_max", [P, CT * GH, NCH])
        top = sb("row_max", [P, CT * GH])
        shift = sb("shift", [P, 2, CT * GH], fp16)
        shiftT = sb("shiftT", [2 * CT * GH, P], fp16)
        OT = sb("OT", [P, CH])
        rcp = sb("row_rcp", [P, CT, GH])

        w_in, stack = new_sem("wqk_in"), new_sem("stack_in")
        mrow = [new_sem("shift_rows_in0"), new_sem("shift_rows_in1")]
        parts_out, shifts_out = new_sem("parts_out"), new_sem("shifts_out")
        rope_in = [new_sem("rope_in0"), new_sem("rope_in1")]
        misc_full, misc_free = new_sem("misc_full"), new_sem("misc_free")
        max_full, max_free = new_sem("piece_full"), new_sem("piece_free")
        s_full, p_full, pv_done = new_sem("scores_full"), new_sem("probs_ready"), new_sem("values_done")
        ot_full, turned, shifts_turned = new_sem("ot_full"), new_sem("turned"), new_sem("shifts_turned")
        rot_done, shift_ready, vg_ready = new_sem("pool2_done"), new_sem("shift_ready"), new_sem("vg_ready")
        dve_done, fills, keys_filled = new_sem("dve2_done"), new_sem("fills_done"), new_sem("keys_filled")
        held, sp_held, pool_held = new_sem("dve2_held"), new_sem("sp2_held"), new_sem("pool2_held")

        def sbank(pr):
            return PSB[:, 2 * pr:2 * pr + 2, :]

        obank = PSB[:, 6, :]
        misc = PSB[:, 7, :]

        def rounds(engine, round_of):
            with engine.Fori(0, G - 1) as g:
                round_of(B * g, 0, g, (1, g))
                round_of(B * g + 1, 1, g, (0, g + 1))
            round_of(B * (G - 1), 0, G - 1, (1, G - 1))
            round_of(B * G - 1, 1, G - 1, None)

        def owner(c, b, g, after):
            return (b, g) if c < NCH else after

        with nc.Block() as block:
            @block.sync
            def _(sp):
                def weights(g):
                    for n, w in enumerate(("q", "k")):
                        sp.dma_start(wq0[:, n, :], io["W" + w][0:P, bass.ds(g * GD, GD)]).then_inc(w_in, 16)
                        sp.dma_start(wq1[0:D1, n, :], io["W" + w][P:D, bass.ds(g * GD, GD)]).then_inc(w_in, 16)
                        sp.dma_start(wq1[D1:D1 + 1, n, :], io["b" + w][bass.ds(g * GD, GD)].rearrange("(o n) -> o n", o=1)).then_inc(w_in, 16)

                def rope_rows(c, g):
                    sp.dma_start(rope[:, c % 2, :, :], io["rope"][bass.ds(g * NCH + c % NCH, 1), :, :, :].rearrange("o p a n -> (o p) a n")).then_inc(rope_in[c % 2], 16)

                def stack_parts(it, c):
                    at, cols = it * NCH + c, slice(c % NCH * CH, (c % NCH + 1) * CH)
                    sp.wait_ge(rot_done, 4 * at + 4)
                    sp.dma_start(io["parts"][c % 2], split[:, :, :]).then_inc(parts_out, 16)
                    if c >= NCH:
                        hold(sp, s_full, 2 * it * ALL_STEPS + 2 * last_use(c), sp_held)
                    sp.wait_ge(parts_out, 16 * at + 16)
                    src = io["parts"][c % 2].rearrange("(k h r) a n -> k a r h n", k=2, h=GH)
                    for dst, k, parts in ((QT, 0, (0, 0, 1)), (KT, 1, (0, 1, 0))):
                        for n, part in enumerate(parts):
                            sp.dma_start(dst[n * HD:(n + 1) * HD, :, cols], src[k, part]).then_inc(stack, 16)

                def shift_rows(it, c):
                    at, cols = it * NCH + c, slice(c % NCH * CH, (c % NCH + 1) * CH)
                    sp.wait_ge(shifts_turned, at + 1)
                    sp.dma_start(io["shifts"][c % 2].rearrange("n (r p) -> (n r) p", p=P), shiftT[:, :]).then_inc(shifts_out, 16)
                    sp.wait_ge(shifts_out, 16 * at + 16)
                    sp.dma_start(QT[SHIFT_ROW:SHIFT_ROW + 2, :, cols],
                                 io["shifts"][c % 2].rearrange("n (h q) -> n h q", h=GH)).then_inc(mrow[c % 2], 16)

                weights(0)
                rope_rows(0, 0)
                rope_rows(1, 0)
                sp.wait_ge(fills, FILLS)
                sp.wait_ge(keys_filled, 2)
                stack_parts(0, 0)
                rope_rows(2, 0)
                stack_parts(0, 1)
                rope_rows(3, 0)
                stack_parts(0, 2)
                shift_rows(0, 0)
                shift_rows(0, 1)

                def round_of(it, b, g, after):
                    stack_parts(it, 3)
                    if after:
                        weights(after[1])
                        rope_rows(4, after[1])
                    shift_rows(it, 2)
                    if after:
                        rope_rows(5, after[1])
                    shift_rows(it, 3)
                    if after:
                        stack_parts(it, 4)
                        rope_rows(6, after[1])
                        stack_parts(it, 5)
                        rope_rows(7, after[1])
                        stack_parts(it, 6)
                        shift_rows(it, 4)
                        shift_rows(it, 5)

                rounds(sp, round_of)

            @block.gpsimd
            def _(pool):
                k = Count(fills)
                k.chain(pool, pool.memset(QT[32:64, :, :], 0.0))
                k.chain(pool, pool.memset(QT[64:P, :, :], 0.0))
                k.chain(pool, pool.memset(VG[:, :, :, HD:32], 0.0))
                k.chain(pool, pool.memset(VG[:, :, :, HD:HD + 1], 1.0))

                def rotate(it, c):
                    at = it * NCH + c
                    k = Count(rot_done, 4 * at)
                    pool.wait_ge(turned, at + 1)
                    k.chain(pool, pool.tensor_tensor(ss[:, :], sh[:, :], rope[:, c % 2, 1, :], ALU.mult))
                    k.on(pool.tensor_tensor(rot[:, :], xc[:, :], ss[:, :], ALU.add))
                    if c:
                        pool.wait_ge(parts_out, 16 * at)
                    k.chain(pool, pool.tensor_tensor(hi, xc[:, :], ss[:, :], ALU.add))
                    k.chain(pool, pool.tensor_tensor(lo, rot[:, :], hi, ALU.subtract))

                def values_of(c, b, g):
                    t = c % NCH * CT
                    pool.tensor_copy(VG[:, t:t + CT, :, 0:HD], VALL[:, b * TB + t:b * TB + t + CT, bass.ds(g * GD, GD)]
                                     .rearrange("p t (h d) -> p t h d", d=HD)).then_inc(vg_ready, 1)

                for c in range(AHEAD):
                    rotate(0, c)
                for c in range(NCH):
                    values_of(c, 0, 0)

                def round_of(it, b, g, after):
                    rotate(it, 3)
                    if after:
                        for c in range(NCH, 2 * NCH):
                            if c < NCH + AHEAD:
                                rotate(it, c)
                            hold(pool, pv_done, it * ALL_STEPS + last_use(c), pool_held)
                            values_of(c, *after)

                rounds(pool, round_of)

            @block.tensor
            def _(pe):
                def run(order, uses, it, b, g, after, misc_base):
                    pieces = pieces_before(order[0][1]) if it is None else pieces_before(2)
                    it = 0 if it is None else it
                    for what, c, n in order:
                        at = it * NCH + c
                        if (what, c) in uses:
                            pe.wait_ge(misc_free, misc_base + uses[what, c] + START)
                        if what == "project":
                            if c % NCH == 0:
                                pe.wait_ge(w_in, (it + c // NCH + 1) * 96)
                            ob = owner(c, b, g, after)[0]
                            cols = slice(ob * S + c % NCH * CH, ob * S + (c % NCH + 1) * CH)
                            pe.matmul(misc, wq0[:, :, :].rearrange("p a n -> p (a n)"), XT0[:, cols], start=True, stop=False)
                            pe.matmul(misc, wq1[:, :, :].rearrange("p a n -> p (a n)"), XT1[:, cols], start=False, stop=True).then_inc(misc_full, 1)
                        elif what == "max":
                            if n == 0:
                                pe.wait_ge(stack, (at + 1) * (16 * STACKS))
                            pe.wait_ge(max_free, it * ALL_PIECES + max(pieces - 1, 0) + START)
                            qt, h, kc, w = piece(c, n)
                            q0, k0 = (c % NCH * CT + qt) * P, kc * CH
                            bank = PSB[:, 4 + pieces % 2, :]
                            mm = pe.matmul(bank[:, 0:w], QT[0:SHIFT_ROW, h, q0:q0 + P], KT[0:SHIFT_ROW, h, k0:k0 + w],
                                           start=True, stop=kc != c % NCH)
                            if kc == c % NCH:
                                mm = pe.matmul(bank[:, w - P:w], mem["identb"][:, :], mem["masks"][:, 0, :], start=False, stop=True)
                            mm.then_inc(max_full, 1)
                            pieces += 1
                        elif what == "shift":
                            pe.wait_ge(shift_ready, at + 1)
                            pe.transpose(misc.bitcast(fp16)[0:2 * CT * GH, 0:P], shift[:, :, :].rearrange("p a n -> p (a n)"),
                                         mem["ident16"][:, :]).then_inc(misc_full, 1)
                        elif what == "scores":
                            j, pr = n
                            step, q0 = steps_before(c) + j, first_query(c, j)
                            if j == 0 and pr == 0:
                                pe.wait_ge(mrow[c % 2], 16 * (it * (NCH // 2) + c // 2) + 16)
                            if step:
                                pe.wait_ge(p_full, it * (2 * ALL_STEPS) + 2 * step - 1 + pr)
                            for h in (2 * pr, 2 * pr + 1):
                                dst = sbank(pr)[:, h % 2, q0:CH]
                                mm = pe.matmul(dst, KT[:, h, j * P:(j + 1) * P], QT[:, h, c * CH + q0:(c + 1) * CH],
                                               start=True, stop=j < CT * c)
                                if j >= CT * c:
                                    mm = pe.matmul(dst[:, 0:P], mem["identb"][:, :], mem["masks"][:, 1, :], start=False, stop=True)
                            mm.then_inc(s_full, 1)
                        elif what == "values":
                            step, q0 = steps_before(c) + n, first_query(c, n)
                            pe.wait_ge(p_full, it * (2 * ALL_STEPS) + 2 * step + 2)
                            if n == 0:
                                if c:
                                    pe.wait_ge(ot_full, at)
                                pe.wait_ge(vg_ready, at + 1)
                            for h in range(GH):
                                mm = pe.matmul(obank[32 * h:32 * h + 32, q0:CH], VG[:, n, h, :], probs[:, step % 2, h, q0:CH],
                                               start=n == 0, stop=n == STEPS[c] - 1)
                            mm.then_inc(pv_done, 1)
                        elif what == "norm":
                            pe.wait_ge(ot_full, at + 1)
                            for t in range(CT):
                                mm = pe.transpose(misc[:, t * P:(t + 1) * P], OT[:, t * P:(t + 1) * P], mem["ident"][:, :])
                            mm.then_inc(misc_full, 1)

                run(OPENING, misc_uses(OPENING), None, 0, 0, None, 0)

                def round_of(it, b, g, after):
                    order = round_order(after)
                    run(order, misc_uses(order), it, b, g, after, it * MISC + MISC_FIRST)

                rounds(pe, round_of)

            @block.scalar
            def _(act):
                def round_of(it, b, g, after):
                    order = round_order(after)
                    uses, misc_base = misc_uses(order), it * MISC + MISC_FIRST
                    for what, c, n in order:
                        if what == "scores":
                            j, pr = n
                            step, q0 = steps_before(c) + j, first_query(c, j)
                            if step >= 2 and pr == 0:
                                act.wait_ge(pv_done, it * ALL_STEPS + step - 1)
                            act.wait_ge(s_full, it * (2 * ALL_STEPS) + 2 * step + pr + 1)
                            act.activation(probs[:, step % 2, 2 * pr:2 * pr + 2, q0:CH], sbank(pr)[:, :, q0:CH], ACT.Exp,
                                           scale=1.0 / HD ** 0.5).then_inc(p_full, 1)
                        elif what == "values" and n == STEPS[c] - 1:
                            act.wait_ge(pv_done, it * ALL_STEPS + steps_before(c + 1))
                            if c:
                                act.wait_ge(misc_full, misc_base + uses["norm", c - 1] + 1)
                            act.activation(OT[:, :], obank, ACT.Copy).then_inc(ot_full, 1)

                rounds(act, round_of)

            @block.vector
            def _(dve):
                dve.memset(KT[32:64, :, :], 1.0).then_inc(keys_filled, 1)
                dve.memset(KT[64:P, :, :], 1.0).then_inc(keys_filled, 1)
                dve.sem_inc(misc_free, START)
                dve.sem_inc(max_free, START)

                def run(order, uses, it, b, g, misc_base, done):
                    k = Count(dve_done, done)
                    pieces = pieces_before(order[0][1]) if it is None else pieces_before(2)
                    it = 0 if it is None else it
                    for what, c, n in order:
                        at = it * NCH + c
                        if what == "rotate":
                            dve.wait_ge(rope_in[c % 2], (it * (NCH // 2) + c // 2) * 16 + 16)
                            if c:
                                dve.wait_ge(rot_done, 4 * at)
                            dve.wait_ge(misc_full, misc_base + uses["project", c] + 1)
                            k.on(dve.tensor_tensor(xc[:, :], misc, rope[:, c % 2, 0, :], ALU.mult))
                            dve.stream_shuffle(sh[:, :], misc, [p ^ 1 for p in range(32)]).then_inc(turned, 1)
                            hold(dve, turned, at + 1, held)
                            dve.sem_inc(misc_free, 1)
                        elif what == "max":
                            qt, h, kc, w = piece(c, n)
                            dve.wait_ge(max_full, it * ALL_PIECES + pieces + 1)
                            dve.tensor_reduce(tops[:, h * CT + qt, kc:kc + 1], PSB[:, 4 + pieces % 2, 0:w], AX.X, ALU.max).then_inc(max_free, 1)
                            pieces += 1
                        elif what == "top":
                            dve.wait_ge(max_free, it * ALL_PIECES + pieces + START)
                            k.chain(dve, dve.tensor_reduce(top[:, :], tops[:, :, 0:c % NCH + 1], AX.X, ALU.max))
                            k.chain(dve, dve.tensor_scalar(shift[:, 0, :], top[:, :], -1.0, None, ALU.mult))
                            dve.scalar_tensor_tensor(out=shift[:, 1, :], in0=top[:, :], scalar=-1.0, in1=shift[:, 0, :],
                                                     op0=ALU.mult, op1=ALU.subtract).then_inc(shift_ready, 1)
                        elif what == "rows":
                            if c:
                                dve.wait_ge(shifts_out, 16 * at)
                            dve.wait_ge(misc_full, misc_base + uses["shift", c] + 1)
                            dve.tensor_copy(shiftT[:, :], misc.bitcast(fp16)[0:2 * CT * GH, 0:P]).then_inc(shifts_turned, 1)
                            hold(dve, shifts_turned, at + 1, held)
                            dve.sem_inc(misc_free, 1)
                        elif what == "divide":
                            dve.wait_ge(misc_full, misc_base + uses["norm", c] + 1)
                            heads = misc.rearrange("p (t h d) -> p t h d", t=CT, h=GH)
                            k.chain(dve, dve.reciprocal(rcp[:, :, :], heads[:, :, :, HD]))
                            dst = AO[:, b * TB + c * CT:b * TB + (c + 1) * CT, bass.ds(g * GD, GD)].rearrange("p t (h d) -> p t h d", d=HD)
                            dve.tensor_tensor(dst, heads[:, :, :, 0:HD], rcp[:, :, :].unsqueeze(3).broadcast_to([P, CT, GH, HD]), ALU.mult).then_inc(misc_free, 1)
                    return k.n

                n = run(OPENING, misc_uses(OPENING), None, 0, 0, 0, 0)
                assert n == DVE2_FIRST, n

                def round_of(it, b, g, after):
                    order = round_order(after)
                    n = run(order, misc_uses(order), it, b, g, it * MISC + MISC_FIRST, it * DVE2 + DVE2_FIRST)
                    assert n == DVE2 or not after, n

                rounds(dve, round_of)


STACKS = 3 * 2
FILLS = 4


GATES = E + 1
DVE3 = 1 + 2 * QUAD


def mix_and_norm(nc, io, mem, new_sem):
    H, AO, XN2, PSB, ident, LG = mem["H"], mem["AO"], mem["VALL"], mem["PSB"], mem["ident"], mem["LG"]
    with ExitStack() as ctx:
        def sb(name, shape, dt=fp32):
            return ctx.enter_context(nc.sbuf_tensor(name, shape, dt))

        wo0, wo1 = sb("wo0", [P, D]), sb("wo1", [D1 + 1, D])
        wg0, wg1 = sb("wg0", [P, GATES]), sb("wg1", [D1 + 1, GATES])
        aq = sb("aq", [P, QUAD, D])
        a0, a1 = sb("a0", [P, QUAD * P]), sb("a1", [D1 + 1, QUAD * P])
        xq = sb("xn2_quad", [P, QUAD, D])
        x0, x1 = sb("x0", [P, QUAD * P]), sb("x1", [D1 + 1, QUAD * P])
        stats, mv = sb("ln2_stats", [P, QUAD, 6]), sb("ln2_mean_var", [P, QUAD, 2])
        var_eps, rstd = sb("ln2_var_eps", [P, QUAD]), sb("ln2_rstd", [P, QUAD])

        w_in, ones_rows = new_sem("wog_in"), new_sem("ones_rows3")
        aq_ready, at_full, a_ready, h_full = new_sem("aq_ready"), new_sem("at_full"), new_sem("a_ready"), new_sem("mix_full")
        dve_done, var_ready, rstd_ready = new_sem("dve3_done"), new_sem("var2_ready"), new_sem("rstd2_ready")
        xq_ready, xq_kept = new_sem("xn2_ready"), new_sem("xn2_kept")
        xt_full, x_ready = new_sem("xt2_full"), new_sem("x2_ready")
        g_full, g_ready, held, act_held = new_sem("gates_full"), new_sem("gates_ready"), new_sem("dve3_held"), new_sem("act3_held")
        at0, at1 = PSB[:, 0, :], PSB[:, 1, :]
        mix = PSB[:, 2:4, :].rearrange("p a (k n) -> p (a k) n", k=2)
        xt0, xt1 = PSB[:, 4, :], PSB[:, 5, :]
        gates = PSB[:, 6, 0:QUAD * 16].rearrange("p (t n) -> p t n", n=16)

        with nc.Block() as block:
            @block.sync
            def _(sp):
                def row(a):
                    return a.rearrange("(o n) -> o n", o=1)
                for dst, src in ((wo0[:, :], io["Wo"][0:P, :]), (wo1[0:D1, :], io["Wo"][P:D, :]),
                                 (wo1[D1:D1 + 1, :], row(io["bo"])),
                                 (wg0[:, 0:E], io["Wg"][0:P, :]), (wg1[0:D1, 0:E], io["Wg"][P:D, :]),
                                 (wg1[D1:D1 + 1, 0:E], row(io["bg"])),
                                 (wg0[:, E:GATES], io["Wm"][0:P].rearrange("(p o) -> p o", o=1)),
                                 (wg1[0:D1, E:GATES], io["Wm"][P:D].rearrange("(p o) -> p o", o=1)),
                                 (wg1[D1:D1 + 1, E:GATES], row(io["bm"]))):
                    sp.dma_start(dst, src).then_inc(w_in, 16)

            @block.gpsimd
            def _(pool):
                with pool.Fori(0, NQ) as q:
                    pool.wait_ge(var_ready, q + 1)
                    pool.tensor_tensor(rstd[:, :], var_eps[:, :], mem["minus_half"][:, 0:QUAD], ALU.pow).then_inc(rstd_ready, 1)

            @block.tensor
            def _(pe):
                pe.wait_ge(w_in, 16 * 9)
                pe.wait_ge(ones_rows, 2)
                pe.sem_inc(xt_full, START)
                def mix_in(q, first=False):
                    pe.wait_ge(a_ready, 2 * q + START)
                    pe.wait_ge(aq_ready, q + 1)
                    for t in range(QUAD):
                        pe.transpose(at0[:, t * P:(t + 1) * P], aq[:, t, 0:P], ident[:, :])
                    for t in range(QUAD):
                        last = pe.transpose(at1[0:D1, t * P:(t + 1) * P], aq[:, t, P:D], ident[:, :])
                    last.then_inc(at_full, 1)
                    pe.wait_ge(a_ready, 2 * q + 2 + START)
                    if not first:
                        pe.wait_ge(dve_done, (q - 1) * DVE3 + 1 + START)
                    for t in range(QUAD):
                        pe.matmul(mix[:, t, 0:D], a0[:, t * P:(t + 1) * P], wo0[:, :], start=True, stop=False)
                        last = pe.matmul(mix[:, t, 0:D], a1[:, t * P:(t + 1) * P], wo1[:, :], start=False, stop=True)
                    last.then_inc(h_full, 1)

                def gate(q):
                    pe.wait_ge(xq_ready, QUAD * (q + 1))
                    pe.wait_ge(x_ready, 2 * q + START)
                    for t in range(QUAD):
                        pe.transpose(xt0[:, t * P:(t + 1) * P], xq[:, t, 0:P], ident[:, :])
                    for t in range(QUAD):
                        last = pe.transpose(xt1[0:D1, t * P:(t + 1) * P], xq[:, t, P:D], ident[:, :])
                    last.then_inc(xt_full, 1)
                    pe.wait_ge(x_ready, 2 * q + 2 + START)
                    pe.wait_ge(g_ready, q + START)
                    for t in range(QUAD):
                        pe.matmul(gates[:, t, 0:GATES], x0[:, t * P:(t + 1) * P], wg0[:, :], start=True, stop=False)
                        last = pe.matmul(gates[:, t, 0:GATES], x1[:, t * P:(t + 1) * P], wg1[:, :], start=False, stop=True)
                    last.then_inc(g_full, 1)

                mix_in(0, first=True)
                with pe.Fori(0, NQ - 1) as q:
                    mix_in(q + 1)
                    gate(q)
                gate(NQ - 1)

            @block.scalar
            def _(act):
                def quad_in(q):
                    act.activation(aq[:, :, :], AO[:, bass.ds(q * QUAD, QUAD), :], ACT.Copy).then_inc(aq_ready, 1)

                def turned_in(q):
                    act.wait_ge(at_full, q + 1)
                    act.activation(a0[:, :], at0, ACT.Copy).then_inc(a_ready, 1)
                    act.activation(a1[0:D1, :], at1[0:D1, :], ACT.Copy).then_inc(a_ready, 1)

                def gates_out(q):
                    act.wait_ge(xt_full, q + 1 + START)
                    act.activation(x0[:, :], xt0, ACT.Copy).then_inc(x_ready, 1)
                    act.activation(x1[0:D1, :], xt1[0:D1, :], ACT.Copy).then_inc(x_ready, 1)
                    hold(act, xq_ready, QUAD * (q + 1), act_held)
                    act.activation(XN2[:, bass.ds(q * QUAD, QUAD), :], xq[:, :, :], ACT.Copy).then_inc(xq_kept, 1)
                    hold(act, g_full, q + 1, act_held)
                    act.activation(LG[:, bass.ds(q * QUAD, QUAD), :], gates[:, :, 0:GATES], ACT.Copy).then_inc(g_ready, 1)

                for sem in (a_ready, x_ready, g_ready, xq_kept):
                    act.sem_inc(sem, START)
                quad_in(0)
                turned_in(0)
                quad_in(1)
                with act.Fori(0, NQ - 2) as q:
                    turned_in(q + 1)
                    quad_in(q + 2)
                    gates_out(q)
                turned_in(NQ - 1)
                gates_out(NQ - 2)
                gates_out(NQ - 1)

            @block.vector
            def _(dve):
                dve.memset(a1[D1:D1 + 1, :], 1.0).then_inc(ones_rows, 1)
                dve.memset(x1[D1:D1 + 1, :], 1.0).then_inc(ones_rows, 1)
                dve.sem_inc(dve_done, START)
                with dve.Fori(0, NQ) as q:
                    k = Count(dve_done, q * DVE3 + START)
                    h = H[:, bass.ds(q * QUAD, QUAD), :]
                    dve.wait_ge(h_full, q + 1)
                    last = k.on(dve.tensor_tensor(h, h, mix[:, :, 0:D], ALU.add))
                    hold(dve, dve_done, last, held)
                    for t in range(QUAD):
                        last = k.on(dve.bn_stats(stats[:, t, :], H[:, bass.ds(q * QUAD + t, 1), :].rearrange("p o d -> p (o d)")))
                    hold(dve, dve_done, last, held)
                    for t in range(QUAD):
                        last = k.on(dve.bn_aggr(mv[:, t, :], stats[:, t, :]))
                    dve.wait_ge(dve_done, last)
                    dve.tensor_scalar(var_eps[:, :], mv[:, :, 1], EPS, None, ALU.add).then_inc(var_ready, 1)
                    dve.wait_ge(xq_kept, q + START)
                    dve.wait_ge(xt_full, q + START)
                    dve.wait_ge(rstd_ready, q + 1)
                    for t in range(QUAD):
                        dve.tensor_scalar(xq[:, t, :], H[:, bass.ds(q * QUAD + t, 1), :].rearrange("p o d -> p (o d)"),
                                          mv[:, t, 0:1], rstd[:, t:t + 1], ALU.subtract, ALU.mult).then_inc(xq_ready, 1)
                    assert k.n == DVE3, k.n


def count_above(dve, mem, above, ranked, b):
    for t in range(TB):
        if t:
            dve.wait_ge(ranked, t)
        at = b * TB + t
        dve.tensor_scalar(above[:, :], mem["score_all"][:, b, :], mem["score"][:, at:at + 1], None, ALU.is_gt, ALU.add,
                          accum_out=mem["rank"][:, at:at + 1]).then_inc(ranked, 1)


def route(nc, io, mem, new_sem):
    XN2, PSB, ident, LG = mem["VALL"], mem["PSB"], mem["ident"], mem["LG"]
    top_p, score, dest = mem["top_p"], mem["score"], mem["dest"]
    logits, z = LG[:, 0:NT, 0:E], LG[:, 0:NT, E]
    with ExitStack() as ctx:
        def sb(name, shape, dt=fp32):
            return ctx.enter_context(nc.sbuf_tensor(name, shape, dt))

        best, less, ex = sb("best", [P, NT]), sb("below_best", [P, NT, E]), sb("exp_logits", [P, NT, E])
        total, ez = sb("exp_sum", [P, NT]), sb("exp_score", [P, NT])
        eq = sb("is_best", [P, NT, E])
        run = [sb("run_a", [P, NT, E]), sb("run_b", [P, NT, E])]
        oh = sb("expert_one_hot", [P, NT, E])
        tot = [sb("tiles_a", [P, NT, E]), sb("tiles_b", [P, NT, E])]
        own = sb("tile_counts", [P, NT, E])
        whole_i, whole = sb("whole_tiles_i", [P, E], i32), sb("whole_tiles", [P, E])
        end = [sb("end_a", [P, E]), sb("end_b", [P, E])]
        base = sb("expert_base", [P, E])
        place = sb("place", [P, NT, E])
        dest_f = sb("dest_f", [P, NT])
        starts_i, starts = sb("tile_starts_i", [1, SLOTS], i32), sb("tile_starts", [1, SLOTS])
        passed = sb("experts_passed", [1, SLOTS, E])
        expert_f = sb("tile_expert_f", [1, SLOTS])
        sT = sb("score_rows_sb", [NT, P])

        above, ranked = sb("above_a", [P, S]), new_sem("ranked_a")
        dve_done, pool_done, ex_ready = new_sem("dve4_done"), new_sem("pool4_done"), new_sem("exps_ready")
        less_ready, oh_ready, ranks_full = new_sem("less_ready"), new_sem("one_hot_ready"), new_sem("ranks_full")
        score_ready, sT_full, sT_ready, s_out = new_sem("score_ready"), new_sem("sT_full"), new_sem("sT_ready"), new_sem("score_out")
        dest_ready, scattered, table_ready = new_sem("dest_ready"), new_sem("scattered"), new_sem("table_ready")
        ranks, totals, st = PSB[:, 0, 0:NT * E].rearrange("p (t e) -> p t e", e=E), PSB[:, 1, 0:NT * E].rearrange("p (t e) -> p t e", e=E), PSB[:, 2, 0:P]
        SB = mem["score_all"]

        with nc.Block() as block:
            @block.vector
            def _(dve):
                k = Count(dve_done)
                k.chain(dve, dve.tensor_reduce(best[:, :], logits, AX.X, ALU.max))
                dve.tensor_tensor(less[:, :, :], logits, best[:, :].unsqueeze(2).broadcast_to([P, NT, E]), ALU.subtract).then_inc(less_ready, 1)
                dve.wait_ge(less_ready, 1)
                k.chain(dve, dve.tensor_scalar(eq[:, :, :], less[:, :, :], 0.0, None, ALU.is_equal))
                now = eq
                for n, s in enumerate((1, 2, 4)):
                    new = run[n % 2]
                    k.on(dve.tensor_copy(new[:, :, 0:s], now[:, :, 0:s]))
                    k.chain(dve, dve.tensor_tensor(new[:, :, s:E], now[:, :, s:E], now[:, :, 0:E - s], ALU.add))
                    now = new
                dve.scalar_tensor_tensor(out=oh[:, :, :], in0=now[:, :, :], scalar=1.0, in1=eq[:, :, :],
                                         op0=ALU.is_equal, op1=ALU.mult).then_inc(oh_ready, 1)
                dve.wait_ge(ex_ready, 2)
                k.chain(dve, dve.tensor_scalar(ez[:, :], ez[:, :], 1.0, None, ALU.add))
                dve.reciprocal(score[:, :], ez[:, :]).then_inc(score_ready, 1)
                k.chain(dve, dve.tensor_reduce(total[:, :], ex[:, :, :], AX.X, ALU.add))
                k.chain(dve, dve.reciprocal(top_p[:, :], total[:, :]))
                dve.wait_ge(ranks_full, 1)
                k.chain(dve, dve.tensor_copy(own[:, :, :], totals))
                now = own
                for n in range(5):
                    s, new = 1 << n, tot[n % 2]
                    k.on(dve.tensor_copy(new[:, 0:s, :], now[:, 0:s, :]))
                    k.chain(dve, dve.tensor_tensor(new[:, s:NT, :], now[:, s:NT, :], now[:, 0:NT - s, :], ALU.add))
                    now = new
                k.chain(dve, dve.tensor_tensor(place[:, :, :], now[:, :, :], own[:, :, :], ALU.subtract))
                k.chain(dve, dve.tensor_tensor(place[:, :, :], place[:, :, :], ranks, ALU.add))
                k.chain(dve, dve.tensor_scalar(whole_i[:, :], now[:, NT - 1, :], float(P - 1), None, ALU.add))
                k.chain(dve, dve.tensor_scalar(whole_i[:, :], whole_i[:, :], 7, 7, ALU.logical_shift_right, ALU.logical_shift_left))
                k.chain(dve, dve.tensor_copy(whole[:, :], whole_i[:, :]))
                now = whole
                for n, s in enumerate((1, 2, 4)):
                    new = end[n % 2]
                    k.on(dve.tensor_copy(new[:, 0:s], now[:, 0:s]))
                    k.chain(dve, dve.tensor_tensor(new[:, s:E], now[:, s:E], now[:, 0:E - s], ALU.add))
                    now = new
                ends = now
                k.chain(dve, dve.tensor_tensor(base[:, :], ends[:, :], whole[:, :], ALU.subtract))
                k.chain(dve, dve.tensor_tensor(place[:, :, :], place[:, :, :], base[:, :].unsqueeze(1).broadcast_to([P, NT, E]), ALU.add))
                k.chain(dve, dve.tensor_tensor(place[:, :, :], place[:, :, :], oh[:, :, :], ALU.mult))
                k.chain(dve, dve.tensor_reduce(dest_f[:, :], place[:, :, :], AX.X, ALU.add))
                dve.tensor_copy(dest[:, :], dest_f[:, :]).then_inc(dest_ready, 1)
                dve.wait_ge(pool_done, 1)
                k.chain(dve, dve.tensor_copy(starts[:, :], starts_i[:, :]))
                k.chain(dve, dve.tensor_tensor(passed[:, :, :], ends[0:1, :].unsqueeze(1).broadcast_to([1, SLOTS, E]),
                                               starts[:, :].unsqueeze(2).broadcast_to([1, SLOTS, E]), ALU.is_le))
                k.chain(dve, dve.tensor_reduce(expert_f[:, :], passed[:, :, :], AX.X, ALU.add))
                dve.tensor_scalar(mem["tile_expert"][:, :], expert_f[:, :], float(E - 1), None, ALU.min).then_inc(table_ready, 1)
                dve.wait_ge(sT_full, 1)
                dve.tensor_copy(sT[:, :], st[0:NT, :]).then_inc(sT_ready, 1)
                dve.wait_ge(s_out, 48)
                count_above(dve, mem, above, ranked, 0)

            @block.scalar
            def _(act):
                act.wait_ge(less_ready, 1)
                act.activation(ex[:, :, :], less[:, :, :], ACT.Exp).then_inc(ex_ready, 1)
                act.activation(ez[:, :], z, ACT.Exp, scale=-1.0).then_inc(ex_ready, 1)

            @block.tensor
            def _(pe):
                pe.wait_ge(oh_ready, 1)
                pe.matmul(ranks, mem["before"][:, :], oh[:, :, :], start=True, stop=True)
                pe.matmul(totals, mem["ones"][:, :], oh[:, :, :], start=True, stop=True).then_inc(ranks_full, 1)
                pe.wait_ge(score_ready, 1)
                pe.transpose(st[0:NT, :], score[:, :], ident[:, :]).then_inc(sT_full, 1)

            @block.gpsimd
            def _(pool):
                pool.iota(starts_i[:, :], pattern=[[P, SLOTS]], base=0, channel_multiplier=0).then_inc(pool_done, 1)
                pool.wait_ge(dest_ready, 1)
                for t in range(NT):
                    pool.indirect_dma_start(io["sorted_x"][:, :], bass.IndirectOffsetOnAxis(dest[:, t:t + 1], 0),
                                            XN2[:, t, :], None).then_inc(scattered, 16)
                pool.wait_ge(scattered, 16 * NT)

            @block.sync
            def _(sp):
                sp.wait_ge(sT_ready, 1)
                sp.dma_start(io["score_rows"].rearrange("b (t p) -> (b t) p", p=P), sT[:, :]).then_inc(s_out, 16)
                sp.wait_ge(s_out, 16)
                for b in range(B):
                    sp.dma_start(SB[:, b, :], io["score_rows"][b:b + 1, :].broadcast_to([P, S])).then_inc(s_out, 16)
                sp.wait_ge(s_out, 48)


HROW = HC // 2 * P


def experts(nc, io, mem, new_sem):
    PSB, ident = mem["PSB"], mem["ident"]
    with ExitStack() as ctx:
        def sb(name, shape, dt=fp32):
            return ctx.enter_context(nc.sbuf_tensor(name, shape, dt))

        w1a, w1b = sb("w1a", [P, 2, HID]), sb("w1b", [D1 + 1, 2, HID])
        w2 = sb("w2", [P, 2, HC, D])
        b2 = sb("b2", [P, 2, D])
        xs = sb("xs", [P, 2, D])
        xt = sb("xs_t", [P, 2, 2, P])
        hid = sb("hidden", [P, 2, HC, P])
        ys = sb("ys", [P, 2, D])

        x_in = [new_sem("x_in0"), new_sem("x_in1")]
        w1_in = [new_sem("w1_in0"), new_sem("w1_in1")]
        w2_in = [new_sem("w2_in0"), new_sem("w2_in1")]
        y_out = [new_sem("y_out0"), new_sem("y_out1")]
        ones_rows, t_full, t_ready = new_sem("ones_rows5"), new_sem("xs_t_full"), new_sem("xs_t_ready")
        up_done, act_done, down_done, y_ready = new_sem("up_done"), new_sem("gelu_done"), new_sem("down_done"), new_sem("y_ready")
        pool_held, y_free = new_sem("pool5_held"), new_sem("y_free")
        sp_held = new_sem("sp5_held")

        def tbank(u):
            return PSB[:, 4 + u, :]

        def ybank(u):
            return PSB[:, 6 + u, 0:D]

        def hbank(u):
            return PSB[:, 2 * u:2 * u + 2, 0:HROW]

        def xrows(s):
            return io["sorted_x"][bass.ds(s * P, P), :]

        with nc.Block() as block:
            @block.sync
            def _(sp):
                def load_x(s, u):
                    sp.dma_start(xs[:, u, :], xrows(s)).then_inc(x_in[u], 16)

                def load_w1(e, u):
                    sp.dma_start(w1a[:, u, :], io["W1"][bass.ds(e, 1), 0:P, :].rearrange("o p n -> (o p) n")).then_inc(w1_in[u], 16)
                    sp.dma_start(w1b[0:D1, u, :], io["W1"][bass.ds(e, 1), P:D, :].rearrange("o p n -> (o p) n")).then_inc(w1_in[u], 16)
                    sp.dma_start(w1b[D1:D1 + 1, u, :], io["b1"][bass.ds(e, 1), :]).then_inc(w1_in[u], 16)

                def load_w2(e, u):
                    sp.dma_start(w2[:, u, :, :], io["W2"][bass.ds(e, 1), :, :].rearrange("o (m p) n -> (o p) m n", p=P)).then_inc(w2_in[u], 16)
                    sp.dma_start(b2[:, u, :], io["b2"][bass.ds(e, 1), :].broadcast_to([P, D])).then_inc(w2_in[u], 16)

                def expert_of(s):
                    return sp.value_load(mem["tile_expert"][0:1, bass.ds(s, 1)], min_val=0, max_val=E - 1)

                for s in range(2):
                    e = expert_of(s)
                    load_x(s, s)
                    load_w1(e, s)
                    load_w2(e, s)
                with sp.Fori(0, SLOTS // 2 - 1) as i:
                    for u in range(2):
                        s = 2 * i + 2 + u
                        e = expert_of(s)
                        hold(sp, t_full, 2 * i + 1 + u, sp_held)
                        load_x(s, u)
                        hold(sp, up_done, 2 * i + 1 + u, sp_held)
                        load_w1(e, u)
                        hold(sp, y_ready, 2 * i + 1 + u, sp_held)
                        load_w2(e, u)

            @block.tensor
            def _(pe):
                def turn(s, u, i):
                    pe.wait_ge(x_in[u], (i + 1) * 16)
                    pe.transpose(tbank(u)[:, 0:P], xs[:, u, 0:P], ident[:, :])
                    pe.transpose(tbank(u)[0:D1, P:2 * P], xs[:, u, P:D], ident[:, :]).then_inc(t_full, 1)

                def up(s, u, i):
                    pe.wait_ge(w1_in[u], (i + 1) * 48)
                    pe.wait_ge(t_ready, 2 * s + 2)
                    for m in range(HC):
                        dst = PSB[:, 2 * u + m // (HC // 2), m % (HC // 2) * P:(m % (HC // 2) + 1) * P]
                        pe.matmul(dst, w1a[:, u, m * P:(m + 1) * P], xt[:, u, 0, :], start=True, stop=False)
                        mm = pe.matmul(dst, w1b[:, u, m * P:(m + 1) * P], xt[0:D1 + 1, u, 1, :], start=False, stop=True)
                    mm.then_inc(up_done, 1)

                def down(s, u, i):
                    pe.wait_ge(w2_in[u], (i + 1) * 32)
                    pe.wait_ge(act_done, s + 1)
                    for m in range(HC):
                        mm = pe.matmul(ybank(u), hid[:, u, m, :], w2[:, u, m, :], start=m == 0, stop=m == HC - 1)
                    mm.then_inc(down_done, 1)

                pe.wait_ge(ones_rows, 2)
                turn(0, 0, 0)
                up(0, 0, 0)
                turn(1, 1, 0)
                with pe.Fori(0, SLOTS // 2 - 1) as i:
                    s = 2 * i
                    up(s + 1, 1, i)
                    turn(s + 2, 0, i + 1)
                    down(s, 0, i)
                    up(s + 2, 0, i + 1)
                    turn(s + 3, 1, i + 1)
                    down(s + 1, 1, i)
                last = SLOTS // 2 - 1
                up(SLOTS - 1, 1, last)
                down(SLOTS - 2, 0, last)
                down(SLOTS - 1, 1, last)

            @block.scalar
            def _(act):
                with act.Fori(0, SLOTS // 2) as i:
                    for u in range(2):
                        act.wait_ge(up_done, 2 * i + u + 1)
                        act.activation(hid[:, u, :, :].rearrange("p (a m) t -> p a (m t)", a=2), hbank(u), ACT.Gelu_apprx_tanh).then_inc(act_done, 1)

            @block.vector
            def _(dve):
                for u in range(2):
                    dve.memset(xt[D1:D1 + 1, u, 1, :], 1.0).then_inc(ones_rows, 1)

                def tile(i, u):
                    s = 2 * i + u
                    dve.wait_ge(t_full, s + 1)
                    dve.tensor_copy(xt[:, u, 0, :], tbank(u)[:, 0:P]).then_inc(t_ready, 1)
                    dve.tensor_copy(xt[0:D1, u, 1, :], tbank(u)[0:D1, P:2 * P]).then_inc(t_ready, 1)

                def finish(s, u, i):
                    dve.wait_ge(y_free, s + 1)
                    dve.wait_ge(down_done, s + 1)
                    dve.tensor_tensor(ys[:, u, :], ybank(u), b2[:, u, :], ALU.add).then_inc(y_ready, 1)

                tile(0, 0)
                with dve.Fori(0, SLOTS // 2 - 1) as i:
                    tile(i, 1)
                    finish(2 * i, 0, i)
                    tile(i + 1, 0)
                    finish(2 * i + 1, 1, i)
                last = SLOTS // 2 - 1
                tile(last, 1)
                finish(SLOTS - 2, 0, last)
                finish(SLOTS - 1, 1, last)

            @block.gpsimd
            def _(pool):
                pool.sem_inc(y_free, 2)
                with pool.Fori(0, SLOTS // 2) as i:
                    for u in range(2):
                        hold(pool, y_ready, 2 * i + u + 1, pool_held)
                        pool.dma_start(io["sorted_y"][bass.ds((2 * i + u) * P, P), :], ys[:, u, :]).then_inc(y_out[u], 16)
                        pool.wait_ge(y_out[u], i * 16 + 16)
                        pool.sem_inc(y_free, 1)
                for u in range(2):
                    pool.wait_ge(y_out[u], SLOTS // 2 * 16)


LEN, WARM = 8, 24
SPAN = 2 * LEN
WIN = SPAN + 2 * WARM
ROUNDS = WARM + LEN


def finish(nc, io, mem, new_sem, out):
    H, PSB, ident = mem["H"], mem["PSB"], mem["ident"]
    Y, FFN = mem["VALL"], mem["AO"]
    top_p, rank, dest = mem["top_p"], mem["rank"], mem["dest"]
    with ExitStack() as ctx:
        def sb(name, shape, dt=fp32):
            return ctx.enter_context(nc.sbuf_tensor(name, shape, dt))

        wv, wo2, fbo = sb("wv_row", [P, D]), sb("feature_rows", [P, 2, D]), sb("feature_bias", [P, D])
        bv, bk = sb("v_bias", [P, 1]), sb("bk_scale_sb", [P, 1])
        prod = sb("v_products", [P, 2, D])
        v, mask = sb("v", [P, NT]), sb("mask", [P, NT])
        vT = sb("vT", [NT, P])
        edge = sb("edge", [B, 2, PAD])
        win = sb("windows", [P, B, WIN])
        drive = sb("drive", [P, ROUNDS, 2, B, 2, 2])
        state = sb("state", [P, ROUNDS + 1, 2, B, 2, 2])
        sq, den, inv = sb("squares", [P, 2, B, 2, 2]), sb("norms", [P, 2, B, 2]), sb("norm_rcp", [P, 2, B, 2])
        turn = sb("turned_state", [P, 2, B, 2, 2])
        sign = sb("signs", [P, B, 2, LEN])
        cr, ci, c2, cd = (sb(n, [P, B, 2, LEN]) for n in ("c_real", "c_imag", "c_square", "c_norm"))
        g = sb("g", [P, 2, B, 2, LEN])
        gT = sb("gT", [NT, 2, P])
        gp = sb("g_tokens", [P, 2, NT])
        row = sb("out_rows", [P, NT, D])

        c_in, gathered = new_sem("c6_in"), new_sem("y_gathered")
        dve_done, tv_full, vT_ready = new_sem("dve6_done"), new_sem("vT_full"), new_sem("vT_ready")
        edge_ready, pot_out, win_in = new_sem("edge_ready"), new_sem("potential_out"), new_sem("windows_in")
        g_ready, g_out, gT_in, gp_full, row_ready, stored = (new_sem(n) for n in (
            "g_ready", "g_out", "gT_in", "gp_full", "row_ready", "stored"))
        v_ready, y_landed = new_sem("v_ready"), new_sem("y_landed")
        above, ranked = sb("above_b", [P, S]), new_sem("ranked_b")
        tb = PSB[:, 0, :]

        with nc.Block() as block:
            @block.sync
            def _(sp):
                def all_rows(a, n):
                    return a.rearrange("(o n) -> o n", o=1).broadcast_to([P, n])
                sp.dma_start(wv[:, :], all_rows(io["fWv"], D)).then_inc(c_in, 16)
                sp.dma_start(wo2[:, :, :].rearrange("p a n -> p (a n)"), all_rows(io["fWo"].rearrange("a n -> (a n)"), 2 * D)).then_inc(c_in, 16)
                sp.dma_start(fbo[:, :], all_rows(io["fbo"], D)).then_inc(c_in, 16)
                sp.dma_start(bv[:, :], all_rows(io["fbv"], 1)).then_inc(c_in, 16)
                sp.dma_start(bk[:, :], all_rows(io["bk_scale"], 1)).then_inc(c_in, 16)
                sp.wait_ge(edge_ready, 3)
                sp.dma_start(io["potential"][:, 0:PAD], edge[:, 0, :]).then_inc(pot_out, 16)
                sp.dma_start(io["potential"][:, PAD + S:PAD + S + PAD], edge[:, 1, :]).then_inc(pot_out, 16)
                sp.wait_ge(vT_ready, 1)
                for b in range(B):
                    sp.dma_start(io["potential"][b, PAD:PAD + S].rearrange("(t p) -> t p", p=P), vT[b * TB:(b + 1) * TB, :]).then_inc(pot_out, 16)
                sp.wait_ge(pot_out, 64)
                for b in range(B):
                    src = bass.AP(tensor=io["potential"].tensor, offset=b * (2 * PAD + S) + PAD - WARM, ap=[[SPAN, P], [1, WIN]])
                    sp.dma_start(win[:, b, :], src).then_inc(win_in, 16)
                sp.wait_ge(g_ready, 2)
                for a in range(2):
                    sp.dma_start(io["green"][a].rearrange("b (p n) -> p b n", p=P), g[:, a, :, :, :].rearrange("p b m r -> p b (m r)")).then_inc(g_out, 16)
                sp.wait_ge(g_out, 32)
                for a in range(2):
                    sp.dma_start(gT[:, a, :], io["green"][a].rearrange("b (t p) -> (b t) p", p=P)).then_inc(gT_in, 16)
                for q in range(NQ):
                    sp.wait_ge(row_ready, QUAD * (q + 1))
                    b, t = divmod(QUAD * q, TB)
                    sp.dma_start(out[b, t * P:(t + QUAD) * P, :].rearrange("(t p) d -> p t d", p=P), row[:, QUAD * q:QUAD * q + QUAD, :]).then_inc(stored, 16)
                sp.wait_ge(stored, 16 * NQ)

            @block.gpsimd
            def _(pool):
                for q in range(NQ):
                    for t in range(QUAD * q, QUAD * q + QUAD):
                        pool.indirect_dma_start(Y[:, t, :], None, io["sorted_y"][:, :],
                                                bass.IndirectOffsetOnAxis(dest[:, t:t + 1], 0)).then_inc(gathered, 16)
                    pool.wait_ge(gathered, 16 * QUAD * (q + 1))
                    pool.sem_inc(y_landed, 1)

            @block.tensor
            def _(pe):
                pe.wait_ge(v_ready, 1)
                pe.transpose(tb[0:NT, 0:P], v[:, :], ident[:, :]).then_inc(tv_full, 1)
                pe.wait_ge(vT_ready, 1)
                pe.wait_ge(gT_in, 32)
                for a in range(2):
                    mm = pe.transpose(tb[:, a * NT:(a + 1) * NT], gT[:, a, :], ident[0:NT, 0:NT])
                mm.then_inc(gp_full, 1)

            @block.vector
            def _(dve):
                k = Count(dve_done)
                dve.memset(edge[:, :, :], 0.0).then_inc(edge_ready, 1)
                dve.wait_ge(edge_ready, 1)
                dve.memset(edge[:, 0, PAD - 1:PAD], 1e18).then_inc(edge_ready, 1)
                dve.memset(edge[:, 1, 0:1], 1e18).then_inc(edge_ready, 1)
                k.on(dve.memset(drive[:, :, :, :, :, 1], 1.0))
                k.on(dve.memset(state[:, 0, :, :, :, 0], 0.0))
                k.on(dve.memset(state[:, 0, :, :, :, 1], 1.0))
                k.on(dve.memset(sign[:, :, :, 0:LEN:2], 1.0))
                k.on(dve.memset(sign[:, :, :, 1:LEN:2], -1.0))
                count_above(dve, mem, above, ranked, 1)
                dve.wait_ge(ranked, TB)
                dve.wait_ge(c_in, 80)
                for t in range(NT):
                    if t % QUAD == 0:
                        dve.wait_ge(y_landed, t // QUAD + 1)
                    if t >= 2:
                        dve.wait_ge(dve_done, k.n - 2)
                    k.on(dve.tensor_scalar(FFN[:, t, :], Y[:, t, :], top_p[:, t:t + 1], None, ALU.mult))
                    dve.wait_ge(dve_done, k.n)
                    k.on(dve.tensor_tensor_reduce(prod[:, t % 2, :], FFN[:, t, :], wv[:, :], 1.0, 0.0, ALU.mult, ALU.add, v[:, t:t + 1]))
                dve.wait_ge(dve_done, k.n)
                k.chain(dve, dve.tensor_scalar(v[:, :], v[:, :], bv[:, 0:1], -V_MAX, ALU.add, ALU.max))
                dve.tensor_scalar(v[:, :], v[:, :], V_MAX, None, ALU.min).then_inc(v_ready, 1)
                dve.wait_ge(tv_full, 1)
                dve.tensor_copy(vT[:, :], tb[0:NT, 0:P]).then_inc(vT_ready, 1)
                k.on(dve.tensor_scalar(fbo[:, :], fbo[:, :], bk[:, 0:1], None, ALU.mult))
                k.on(dve.tensor_scalar(wo2[:, :, :], wo2[:, :, :], bk[:, 0:1], None, ALU.mult))
                k.on(dve.tensor_scalar(mask[:, :], rank[:, :], float(KEEP), None, ALU.is_lt))
                k.chain(dve, dve.tensor_tensor(row[:, :, :], H[:, :, :], FFN[:, :, :], ALU.add))
                k.chain(dve, dve.tensor_tensor(row[:, :, :], row[:, :, :], fbo[:, :].unsqueeze(1).broadcast_to([P, NT, D]), ALU.add))
                dve.wait_ge(win_in, 32)
                for m in range(2):
                    for par in range(2):
                        f = win[:, :, LEN * m + par:LEN * m + ROUNDS:2]
                        k.on(dve.tensor_scalar(drive[:, par::2, 0, :, m, 0], f.rearrange("p b k -> p k b"), 1.0 - 2 * par, None, ALU.mult))
                        top = LEN * m + WARM + ROUNDS - 1 - par
                        for kk in range(ROUNDS // 2):
                            last = k.on(dve.tensor_scalar(drive[:, par + 2 * kk, 1, :, m, 0], win[:, :, top - 2 * kk], 1.0 - 2 * par, None, ALU.mult))
                dve.wait_ge(dve_done, last)
                for s in range(ROUNDS):
                    now = state[:, s, :, :, :, :]
                    k.chain(dve, dve.tensor_tensor(sq[:, :, :, :, :], now, now, ALU.mult))
                    k.chain(dve, dve.tensor_tensor(den[:, :, :, :], sq[:, :, :, :, 0], sq[:, :, :, :, 1], ALU.add))
                    k.chain(dve, dve.reciprocal(inv[:, :, :, :], den[:, :, :, :]))
                    k.chain(dve, dve.tensor_tensor(turn[:, :, :, :, :], now, inv[:, :, :, :].unsqueeze(4).broadcast_to([P, 2, B, 2, 2]), ALU.mult))
                    k.chain(dve, dve.tensor_tensor(state[:, s + 1, :, :, :, :], turn[:, :, :, :, :], drive[:, s, :, :, :, :], ALU.add))
                for r in range(LEN):
                    f, w = state[:, WARM + 1 + r, 0, :, :, :], state[:, ROUNDS - r, 1, :, :, :]
                    k.on(dve.tensor_tensor(cr[:, :, :, r], f[:, :, :, 0], w[:, :, :, 0], ALU.subtract))
                    k.on(dve.scalar_tensor_tensor(out=ci[:, :, :, r], in0=f[:, :, :, 1], scalar=-1.0, in1=w[:, :, :, 1], op0=ALU.add, op1=ALU.add))
                dve.wait_ge(dve_done, k.n)
                k.chain(dve, dve.tensor_tensor(cr[:, :, :, :], cr[:, :, :, :], sign[:, :, :, :], ALU.mult))
                k.chain(dve, dve.tensor_tensor(cr[:, :, :, :], cr[:, :, :, :], win[:, :, WARM:WARM + SPAN].rearrange("p b (m r) -> p b m r", m=2), ALU.subtract))
                k.chain(dve, dve.tensor_tensor(c2[:, :, :, :], cr[:, :, :, :], cr[:, :, :, :], ALU.mult))
                k.chain(dve, dve.tensor_tensor(cd[:, :, :, :], ci[:, :, :, :], ci[:, :, :, :], ALU.mult))
                k.chain(dve, dve.tensor_tensor(cd[:, :, :, :], cd[:, :, :, :], c2[:, :, :, :], ALU.add))
                k.chain(dve, dve.reciprocal(cd[:, :, :, :], cd[:, :, :, :]))
                dve.tensor_tensor(g[:, 0, :, :, :], cr[:, :, :, :], cd[:, :, :, :], ALU.mult).then_inc(g_ready, 1)
                dve.tensor_tensor(g[:, 1, :, :, :], ci[:, :, :, :], cd[:, :, :, :], ALU.mult).then_inc(g_ready, 1)
                dve.wait_ge(gp_full, 1)
                for a in range(2):
                    last = k.on(dve.tensor_tensor(gp[:, a, :], tb[:, a * NT:(a + 1) * NT], mask[:, :], ALU.mult))
                dve.wait_ge(dve_done, last)
                k.chain(dve, dve.tensor_scalar(gp[:, :, :], gp[:, :, :], -FEAT_CLAMP, FEAT_CLAMP, ALU.max, ALU.min))
                for t in range(NT):
                    k.chain(dve, dve.scalar_tensor_tensor(out=row[:, t, :], in0=wo2[:, 0, :], scalar=gp[:, 0, t:t + 1], in1=row[:, t, :], op0=ALU.mult, op1=ALU.add))
                    dve.scalar_tensor_tensor(out=row[:, t, :], in0=wo2[:, 1, :], scalar=gp[:, 1, t:t + 1], in1=row[:, t, :], op0=ALU.mult, op1=ALU.add).then_inc(row_ready, 1)


def lm_tower(nc, io, out):
    with ExitStack() as c:
        def sb(name, shape, dt=fp32):
            return c.enter_context(nc.sbuf_tensor(name, shape, dt))

        def new_sem(name):
            return c.enter_context(nc.semaphore(name))

        for name, shape, dt in (("sorted_x", [SLOTS * P, D], fp32), ("sorted_y", [SLOTS * P, D], fp32),
                                ("score_rows", [B, S], fp32), ("potential", [B, PAD + S + PAD], fp32),
                                ("green", [2, B, S], fp32), ("parts", [2, P, 2, CH], fp16), ("shifts", [2, 2, CT * GH * P], fp16)):
            io[name] = nc.dram_tensor(name, shape, dt, kind="Internal").ap()
        mem = {
            "H": sb("H", [P, NT, D]),
            "VALL": sb("VALL", [P, NT, D]),
            "AO": sb("AO", [P, NT, D]),
            "ident": sb("ident", [P, P]), "ident16": sb("ident16", [P, P], fp16), "identb": sb("identb", [P, P], bf16),
            "masks": sb("masks", [P, 2, P], bf16), "minus_half": sb("minus_half", [P, NT]),
            "before": sb("before", [P, P]), "ones": sb("ones", [P, P]),
            "PSB": c.enter_context(nc.psum_tensor("PSB", [P, 8, 512], fp32)),
        }
        with ExitStack() as a:
            mem["XT0"] = a.enter_context(nc.sbuf_tensor("XT0", [P, N], fp32))
            mem["XT1"] = a.enter_context(nc.sbuf_tensor("XT1", [D1 + 1, N], fp32))
            embed_and_project_values(nc, io, mem, new_sem)
            attention(nc, io, mem, new_sem)
        mem["LG"] = sb("LG", [P, NT, GATES])
        for name in ("top_p", "score", "rank"):
            mem[name] = sb(name, [P, NT])
        mem["dest"] = sb("dest", [P, NT], i32)
        mem["tile_expert"] = sb("tile_expert", [1, SLOTS], i32)
        mem["score_all"] = sb("score_all", [P, B, S])
        mix_and_norm(nc, io, mem, new_sem)
        route(nc, io, mem, new_sem)
        experts(nc, io, mem, new_sem)
        finish(nc, io, mem, new_sem, out)


PAD = 32


_INS = {"x": "x", "seg": "mask_BS_i2_0", "tok": "L0_tok_token_table", "segm": "L0_tok_segm_table",
        "Wq": "L0_attn_Wq", "bq": "L0_attn_bq", "Wk": "L0_attn_Wk", "bk": "L0_attn_bk",
        "Wv": "L0_attn_Wv", "bv": "L0_attn_bv", "Wo": "L0_attn_Wo", "bo": "L0_attn_bo",
        "Wg": "L0_ffn_Wg", "bg": "L0_ffn_bg", "W1": "L0_ffn_W1", "b1": "L0_ffn_b1",
        "W2": "L0_ffn_W2", "b2": "L0_ffn_b2", "fWv": "L0_ffn_Wv", "fbv": "L0_ffn_bv",
        "Wm": "L0_ffn_Wm", "bm": "L0_ffn_bm", "fWo": "L0_ffn_Wo", "fbo": "L0_ffn_bo",
        "bk_scale": "L0_ffn_bk_scale"}


def shape_constants():
    import numpy as np
    f = np.float32
    pos = np.arange(S, dtype=f)[:, None]
    ids = np.arange(D, dtype=f)
    angle = pos / np.power(10000.0, (np.floor(ids / f(2)) * f(2) / f(D)).astype(np.float64)).astype(f)[None, :]
    table = np.where(np.arange(D) % 2 == 0, np.sin(angle.astype(np.float64)), np.cos(angle.astype(np.float64))).astype(f)
    half = np.arange(D // 2, dtype=f) * f(2) / f(D)
    turn = pos * (f(1) / np.power(10000.0, half.astype(np.float64)).astype(f))[None, :]
    cos = np.repeat(np.cos(turn.astype(np.float64)), 2, 1).T.astype(f)
    sin = np.repeat(np.sin(turn.astype(np.float64)), 2, 1).T.astype(f)
    sin[0::2] *= -1
    rope = np.stack([cos, sin], 1).reshape(G, 1, GD, 2, NCH, CH)
    rope = np.broadcast_to(rope, (G, 2, GD, 2, NCH, CH)).transpose(0, 4, 1, 2, 3, 5).reshape(G * NCH, P, 2, CH)
    return {"pos": np.ascontiguousarray(table.reshape(TB, P, D).transpose(1, 0, 2)), "rope": np.ascontiguousarray(rope)}


def kernel(**inputs):
    import numpy as _np
    import concourse.bacc as _bacc
    from concourse import mybir as _mybir
    from concourse.bass_utils import run_bass_kernel_spmd as _run

    nc = _bacc.Bacc("TRN2", target_bir_lowering=False, num_devices=1)
    arrays, io = {}, {}
    given = {name: _np.ascontiguousarray(inputs[source]) for name, source in _INS.items()}
    for name, a in {**given, **shape_constants()}.items():
        a = a.reshape(a.shape or (1,))
        arrays[f"in_{name}"] = a
        io[name] = nc.dram_tensor(f"in_{name}", a.shape, _mybir.dt.from_np(a.dtype), kind="ExternalInput").ap()
    out = nc.dram_tensor("out_h", [B, S, D], _mybir.dt.float32, kind="ExternalOutput").ap()
    lm_tower(nc, io, out)
    r = _run(nc, [arrays], core_ids=[0])
    return r.results[0]["out_h"]
```
